# Optimizing a Trainium2 kernel written in Bass

```python
import numpy as np
import jax
import jax.numpy as jnp

def _softmax(x, axis=-1):
    return jax.nn.softmax(x, axis=axis)

def _gelu(x):
    return jax.nn.gelu(x, approximate=True)

def _silu(x):
    return jax.nn.silu(x)

def _sigmoid(x):
    return jax.nn.sigmoid(x)

def _layernorm(x, axis=-1, eps=1e-05):
    m = jnp.mean(x, axis=axis, keepdims=True)
    v = jnp.var(x, axis=axis, keepdims=True)
    return (x - m) / jnp.sqrt(v + eps)

def _scatter_add(tgt, idx, src, axis=0):
    return tgt.at[idx].add(src)

def _segment_sum(src, seg, n):
    return jax.ops.segment_sum(src, seg, n)
kernel_name = 'mk_flamingo_gated_d1_seqx_r4_039264'

def setup_inputs(seed: int=0):
    np.random.seed(seed)
    _w = jnp.asarray

    def _rec_inputs():
        import jax
        import jax.numpy as jnp
        _rk = jax.random.key(seed)
        x = -0.000125 + 0.9999 * jax.random.normal(jax.random.fold_in(_rk, 1), (4, 512, 512), jnp.float32)
        _lenS = 512 - jax.random.randint(jax.random.fold_in(_rk, 7), (4,), 0, max(1, 512 // 4) + 1, jnp.int32)
        _lenS2 = 512 - jax.random.randint(jax.random.fold_in(_rk, 8), (4,), 0, max(1, 512 // 4) + 1, jnp.int32)
        itok_BxS_13_99985 = jax.random.randint(jax.random.fold_in(_rk, 11), (4, 512), 13, 99986, jnp.int32)
        _ctx_2048P = jax.random.normal(jax.random.fold_in(_rk, 12), (4, 16, 512), jnp.float32)
        _ctx_2048c = jax.random.dirichlet(jax.random.fold_in(_rk, 512), 0.3 * jnp.ones((16,), jnp.float32), (4, 512))
        _ctx_2048t = jnp.einsum('bsk,bkd->bsd', _ctx_2048c, _ctx_2048P)
        _ctx_2048t = _ctx_2048t * jax.lax.rsqrt(jnp.mean(jnp.square(_ctx_2048t)) + 1e-12) * 0.953939
        ctx_2048 = 6.82029e-06 + 0.0200006 * (_ctx_2048t + 0.3 * jax.random.normal(jax.random.fold_in(_rk, 612), (4, 512, 512), jnp.float32))
        _g = jax.random.normal(jax.random.fold_in(_rk, 9001), (2, 1), jnp.float32)
        _g = jnp.sign(_g) * jnp.maximum(jnp.abs(_g), 1.0) + (_g == 0) * 1.0
        g_xattn = _g[0]
        g_ffn = _g[1]
        return (x, itok_BxS_13_99985, ctx_2048, g_xattn, g_ffn)
    x, itok_BxS_13_99985, ctx_2048, g_xattn, g_ffn = _rec_inputs()

    def _L0_xattn_setup():
        import jax, jax.numpy as jnp
        import numpy as np
        B, S, D = (4, 1024, 512)
        E = 4
        F = 2048 // E
        VOCAB = 25000
        key = jax.random.key(seed)
        k1, k2, k3, k4, k5 = jax.random.split(key, 5)
        hidden_states = jax.random.normal(k1, (B, S, D), dtype=jnp.float32)
        token_ids = jax.random.randint(k2, (B, S), 0, VOCAB, dtype=jnp.int64)
        Wg = jax.random.normal(k3, (E, F, D), dtype=jnp.float32) * 0.02
        Wu = jax.random.normal(k4, (E, F, D), dtype=jnp.float32) * 0.02
        Wd = jax.random.normal(k5, (E, D, F), dtype=jnp.float32) * 0.02
        return {'hidden_states': hidden_states, 'token_ids': token_ids, 'Wg': Wg, 'Wu': Wu, 'Wd': Wd}
    _L0_xattn_all = _L0_xattn_setup()
    _L0_xattn_in = {k: v for k, v in _L0_xattn_all.items() if k in ()}
    del _L0_xattn_all

    def _L0_ffn_setup():
        import jax, jax.numpy as jnp
        import numpy as np
        B, S, D, E, R, TOP_K = (4, 1024, 512, 6, 16, 2)
        key = jax.random.key(seed)
        ks = jax.random.split(key, 9)
        scale = 0.02
        return {'x': jax.random.normal(ks[0], (B, S, D), dtype=jnp.float32), 'W_base': jax.random.normal(ks[1], (D, D), dtype=jnp.float32) * scale, 'b_base': jax.random.normal(ks[2], (D,), dtype=jnp.float32) * scale, 'A_s': jax.random.normal(ks[3], (D, R), dtype=jnp.float32) * scale, 'B_s': jax.random.normal(ks[4], (R, D), dtype=jnp.float32) * scale, 'A_r': jax.random.normal(ks[5], (E, D, R), dtype=jnp.float32) * scale, 'B_r': jax.random.normal(ks[6], (E, R, D), dtype=jnp.float32) * scale, 'W_router': jax.random.normal(ks[7], (D, E), dtype=jnp.float32) * scale, 'b_router': jax.random.normal(ks[8], (E,), dtype=jnp.float32) * scale}
    _L0_ffn_all = _L0_ffn_setup()
    _L0_ffn_in = {k: v for k, v in _L0_ffn_all.items() if k in ('W_base', 'b_base', 'A_s', 'B_s', 'A_r', 'B_r', 'W_router', 'b_router')}
    del _L0_ffn_all
    return {'x': x, 'itok_BxS_13_99985': itok_BxS_13_99985, 'ctx_2048': ctx_2048, 'g_xattn': g_xattn, 'g_ffn': g_ffn, 'L0_ffn_W_base': _L0_ffn_in['W_base'], 'L0_ffn_b_base': _L0_ffn_in['b_base'], 'L0_ffn_A_s': _L0_ffn_in['A_s'], 'L0_ffn_B_s': _L0_ffn_in['B_s'], 'L0_ffn_A_r': _L0_ffn_in['A_r'], 'L0_ffn_B_r': _L0_ffn_in['B_r'], 'L0_ffn_W_router': _L0_ffn_in['W_router'], 'L0_ffn_b_router': _L0_ffn_in['b_router']}

def reference(x, itok_BxS_13_99985, ctx_2048, g_xattn, g_ffn, L0_ffn_W_base, L0_ffn_b_base, L0_ffn_A_s, L0_ffn_B_s, L0_ffn_A_r, L0_ffn_B_r, L0_ffn_W_router, L0_ffn_b_router):
    import jax
    import jax.numpy as jnp

    def _L0_xattn_ref(hidden_states, token_ids, Wg, Wu, Wd):
        import jax, jax.numpy as jnp
        import numpy as np
        B, S, D = (4, 1024, 512)
        E = 4
        F = 2048 // E
        VOCAB = 25000
        tokens_per_expert = VOCAB // E
        tid = jnp.clip(token_ids, 0, VOCAB - 1)
        expert_ids = jnp.minimum(tid // tokens_per_expert, E - 1)
        out = jnp.zeros_like(hidden_states)
        for e in range(E):
            g = jax.nn.silu(jnp.einsum('bsd,fd->bsf', hidden_states, Wg[e]))
            u = jnp.einsum('bsd,fd->bsf', hidden_states, Wu[e])
            y = jnp.einsum('bsf,df->bsd', g * u, Wd[e])
            out = jnp.where((expert_ids == e)[..., None], y, out)
        return out

    def _L0_ffn_ref(x, W_base, b_base, A_s, B_s, A_r, B_r, W_router, b_router):
        import jax, jax.numpy as jnp
        import numpy as np
        B, S, D, E, R, TOP_K = (4, 1024, 512, 6, 16, 2)
        base_out = jax.lax.stop_gradient(jnp.einsum('bsd,df->bsf', x, W_base) + b_base)
        shared_out = jnp.einsum('bsr,rf->bsf', jnp.einsum('bsd,dr->bsr', x, A_s), B_s)
        gates = jax.nn.softmax(jnp.einsum('bsd,de->bse', x, W_router) + b_router, axis=-1)
        topk_w, topk_i = jax.lax.top_k(gates, TOP_K)
        w_per_e = jnp.sum(topk_w[..., None] * jax.nn.one_hot(topk_i, E, dtype=x.dtype), axis=2)
        h = jnp.einsum('bsd,edr->bser', x, A_r)
        hw = h * w_per_e[..., None]
        routed_out = jnp.einsum('bser,erf->bsf', hw, B_r)
        return base_out + shared_out + routed_out
    x = x + jnp.tanh(g_xattn[0]) * _L0_xattn_ref(_layernorm(x, axis=-1), itok_BxS_13_99985, ctx_2048, ctx_2048, ctx_2048)
    x = x + jnp.tanh(g_ffn[0]) * _L0_ffn_ref(_layernorm(x, axis=-1), L0_ffn_W_base, L0_ffn_b_base, L0_ffn_A_s, L0_ffn_B_s, L0_ffn_A_r, L0_ffn_B_r, L0_ffn_W_router, L0_ffn_b_router)
    return x

_drawn_inputs = setup_inputs


def setup_inputs(seed=0):
    import zlib

    import numpy as np

    out = dict(_drawn_inputs(seed))
    spreads = {}
    factors = {'L0_ffn_b_base': 3.289,
     'L0_ffn_A_r': 5.225,
     'L0_ffn_B_r': 5.196,
     'L0_ffn_W_router': 6.275,
     'L0_ffn_b_router': 8.0}
    for name, (base, spread) in spreads.items():
        noise = np.random.default_rng([zlib.crc32(name.encode()), seed]).standard_normal(out[name].shape)
        drawn = base * np.exp(spread * noise) if base else spread * noise
        out[name] = jnp.asarray(drawn.astype(out[name].dtype))
    for name, factor in factors.items():
        out[name] = (out[name] * factor).astype(out[name].dtype)
    return out
```

```python
from contextlib import ExitStack

import concourse.bass as bass
from concourse import mybir

ALU = mybir.AluOpType
ACT = mybir.ActivationFunctionType
AX = mybir.AxisListType
F32 = mybir.dt.float32
F32R = mybir.dt.float32r
F16 = mybir.dt.float16
I32 = mybir.dt.int32

P = 128
VOCAB = 25000
EPS = 1e-5
TOP_K = 2
EXTRA_AT = 12


def build_block(nc, x, ids, ct, gates, w_ffn, w_up, b_router, out):
    N, D = x.shape
    S = ct.shape[0]
    KC = D // P
    TILES = N // P
    EXTRAS = S - 1
    ITEMS = TILES + EXTRAS
    TPP = N // P
    PER_EXPERT = VOCAB // S
    E = b_router.shape[0]
    LORA = w_up.shape[0] - 1
    R = LORA // (E + 1)
    WN = w_ffn.shape[1]
    NA = (WN // 2 + 1) // 2 * 2
    NB = WN - NA
    BB = D - NA
    HR = BB + LORA
    assert NA <= 512 and NB <= 512 and LORA + 1 <= P and ITEMS == 19 and TILES == 16

    def tile_position(t):
        return t if t < EXTRA_AT else t + EXTRAS

    with ExitStack() as ctx:
        def sb(name, shape, dt=F32):
            return ctx.enter_context(nc.sbuf_tensor(name, shape, dt))

        def bank(name):
            return ctx.enter_context(nc.psum_tensor(name, [P, 512], F32))

        def sem(name):
            return ctx.enter_context(nc.semaphore(name))

        xg = sb("xg", [P, ITEMS * D])
        ct_split = sb("ct_split", [P, S * KC * 2 * D], F32R)
        ct_stage = sb("ct_stage", [P, 2, KC, D])
        w_stage = sb("w_stage", [P, KC, WN])
        w_split = sb("w_split", [P, KC, 2, WN], F32R)
        up_stage = sb("up_stage", [P, D])
        up_split = sb("up_split", [P, 2, D], F32R)
        h = sb("h", [P, D])
        hT = sb("hT", [P, 2, D], F32R)
        silu = sb("silu", [P, D])
        act = sb("act", [P, D])
        actT = sb("actT", [P, 2, D], F32R)
        h2T = sb("h2T", [P, 2, 2, D], F32R)
        hw = sb("hw", [P, P])
        hwT = sb("hwT", [P, 2, P], F32R)
        bn = sb("bn", [P, 6])
        stats = sb("stats", [P, 2])
        rstd = sb("rstd", [P, 1])
        var_eps = sb("var_eps", [P, 1])
        minus_half = sb("minus_half", [P, 1])
        ident = sb("ident", [P, P])
        before = sb("before", [P, P], F16)
        ones = sb("ones", [P, P], F16)
        first_row = sb("first_row", [P, P], F16)
        iota_row = sb("iota_row", [P, P], F16)
        token_no = sb("token_no", [P, TPP])
        scan_keep = sb("scan_keep", [P, S * TPP])
        ids_sb = sb("ids_sb", [P, TPP], I32)
        at_least = sb("at_least", [P, S + 1, TPP])
        onehot = sb("onehot", [P, S, TPP])
        rank = sb("rank", [P, S, TPP])
        totals = sb("totals", [P, S], F16)
        totals_before = sb("totals_before", [P, S], F16)
        scan_ones = sb("scan_ones", [P, S])
        no_key = sb("no_key", [P, 2, TPP])
        slot1 = sb("slot1", [P, TPP])
        slot = sb("slot", [P, TPP], I32)
        slot_lo = sb("slot_lo", [P, TPP], I32)
        slot_tile = sb("slot_tile", [P, TPP], I32)
        tile_starts = sb("tile_starts", [P, TILES - 1])
        begun = sb("begun", [P, EXTRAS, TILES - 1])
        item_tile = sb("item_tile", [P, ITEMS])
        in_item = sb("in_item", [P, TPP, ITEMS])
        lo_onehot = sb("lo_onehot", [P, TPP, P], F16)
        item_vals = sb("item_vals", [P, TPP, 2, ITEMS], F16)
        row_index = sb("row_index", [P, ITEMS], I32)
        row_key = sb("row_key", [P, ITEMS], F16)
        item_key = sb("item_key", [P, ITEMS])
        extra_key = sb("extra_key", [P, EXTRAS])
        starts_inside = sb("starts_inside", [P, EXTRAS])
        gate_mask = sb("gate_mask", [P, ITEMS])
        past_extras = sb("past_extras", [P, ITEMS])
        key_table = sb("key_table", [P, ITEMS], I32)
        target_table = sb("target_table", [P, ITEMS], I32)
        gates_raw = sb("gates_raw", [P, 2])
        gates_t = sb("gates_t", [P, 2])
        br = sb("br", [P, E])
        logits = sb("logits", [P, E])
        neg_max = sb("neg_max", [P, 1])
        expd = sb("expd", [P, E])
        exp_sum = sb("exp_sum", [P, 1])
        exp_inv = sb("exp_inv", [P, 1])
        pair_diff = sb("pair_diff", [P, E, E])
        pair_least = sb("pair_least", [P, E, E])
        beats = sb("beats", [P, E, E])
        beaten_by = sb("beaten_by", [P, E])
        chosen = sb("chosen", [P, E])
        weights = sb("weights", [P, E + 1])

        z_ps, hT_ps, actT_ps, y_ps = bank("z_ps"), bank("hT_ps"), bank("actT_ps"), bank("y_ps")
        ffn_a = [bank("ffn_a0"), bank("ffn_a1")]
        ffn_b = [bank("ffn_b0"), bank("ffn_b1")]
        hwT_ps = actT_ps
        sort_ps, perm_ps, lead_ps = ffn_a[0], ffn_a[1], ffn_b[0]

        ids_loaded, gates_loaded, br_loaded = sem("ids_loaded"), sem("gates_loaded"), sem("br_loaded")
        ct_loaded = [sem(f"ct_loaded{s}") for s in range(S)]
        w_loaded, up_loaded = sem("w_loaded"), sem("up_loaded")
        x_landed = [sem(f"x_landed{q}") for q in range(ITEMS)]
        x_ready = sem("x_ready")
        out_stored = sem("out_stored")
        consts_ready = sem("consts_ready")
        pool_step = sem("pool_step")
        dve_step = sem("dve_step")
        gates_ready = sem("gates_ready")
        totals_ready, bases_done = sem("totals_ready"), sem("bases_done")
        perm_in_ready, perm_done = sem("perm_in_ready"), sem("perm_done")
        rows_ready, keys_ready, lead_done, tables_ready = (
            sem("rows_ready"), sem("keys_ready"), sem("lead_done"), sem("tables_ready"))
        ct_hi_ready, ct_lo_ready = sem("ct_hi_ready"), sem("ct_lo_ready")
        w_hi_ready, w_lo_ready = sem("w_hi_ready"), sem("w_lo_ready")
        stats_ready, rstd_ready, h_ready = sem("stats_ready"), sem("rstd_ready"), sem("h_ready")
        hT_done, hT_hi_ready, hT_lo_ready = sem("hT_done"), sem("hT_hi_ready"), sem("hT_lo_ready")
        z_done, silu_ready, act_ready = sem("z_done"), sem("silu_ready"), sem("act_ready")
        actT_done, actT_hi_ready, actT_lo_ready = (
            sem("actT_done"), sem("actT_hi_ready"), sem("actT_lo_ready"))
        y_done, x2_ready = sem("y_done"), sem("x2_ready")
        stats2_ready, rstd2_ready, h2_ready = sem("stats2_ready"), sem("rstd2_ready"), sem("h2_ready")
        h2T_done, h2T_hi_ready, h2T_lo_ready = sem("h2T_done"), sem("h2T_hi_ready"), sem("h2T_lo_ready")
        ffn_done, max_ready, exp_ready = sem("ffn_done"), sem("max_ready"), sem("exp_ready")
        hw_ready, hwT_done, hwT_hi_ready, hwT_lo_ready = (
            sem("hw_ready"), sem("hwT_done"), sem("hwT_hi_ready"), sem("hwT_lo_ready"))
        up_done, out_ready = sem("up_done"), sem("out_ready")
        bn_ready, bn2_ready = sem("bn_ready"), sem("bn2_ready")
        router_step = sem("router_step")
        block = ctx.enter_context(nc.Block())

        CONSTS = 12

        def cols(tensor, position, width=D):
            return tensor[:, bass.ds(position * width, width)]

        @block.sync
        def _(sp):
            sp.dma_start(ids_sb[:], ids.rearrange("(p c) -> p c", c=TPP)).then_inc(ids_loaded, 16)
            sp.dma_start(gates_raw[:], gates.partition_broadcast(P)).then_inc(gates_loaded, 16)
            for s in range(S):
                if s >= 2:
                    sp.wait_ge(ct_hi_ready, s - 1)
                    sp.wait_ge(ct_lo_ready, s - 1)
                sp.dma_start(ct_stage[:, s % 2],
                             ct[s].rearrange("(k p) n -> p k n", p=P)).then_inc(ct_loaded[s], 16)
            sp.dma_start(w_stage[:], w_ffn.rearrange("(k p) n -> p k n", p=P)).then_inc(w_loaded, 16)
            sp.wait_ge(consts_ready, CONSTS)
            sp.dma_start(up_stage[0:LORA + 1, :], w_up).then_inc(up_loaded, 16)
            sp.dma_start(br[:], b_router.partition_broadcast(P)).then_inc(br_loaded, 16)
            for q in range(ITEMS):
                sp.wait_ge(x_landed[q], 16)
                sp.sem_inc(x_ready, 1)
            sp.wait_ge(out_stored, 16 * TILES)

        @block.gpsimd
        def _(pool):
            nc.gpsimd.memset(before[:], 1.0).then_inc(pool_step, 1)
            nc.gpsimd.memset(scan_keep[:], 1.0).then_inc(pool_step, 1)
            nc.gpsimd.iota(iota_row[:], [[1, P]], base=0, channel_multiplier=0,
                           allow_small_or_imprecise_dtypes=True).then_inc(consts_ready, 1)
            nc.gpsimd.iota(no_key[:, 0, :], [[1, TPP]], base=0, channel_multiplier=TPP,
                           allow_small_or_imprecise_dtypes=True).then_inc(consts_ready, 1)
            nc.gpsimd.iota(tile_starts[:], [[P, TILES - 1]], base=P, channel_multiplier=0,
                           allow_small_or_imprecise_dtypes=True).then_inc(consts_ready, 1)
            nc.gpsimd.iota(item_tile[:, 0:EXTRA_AT], [[1, EXTRA_AT]], base=0, channel_multiplier=0,
                           allow_small_or_imprecise_dtypes=True).then_inc(consts_ready, 1)
            nc.gpsimd.iota(item_tile[:, EXTRA_AT + EXTRAS:], [[1, TILES - EXTRA_AT]], base=EXTRA_AT,
                           channel_multiplier=0,
                           allow_small_or_imprecise_dtypes=True).then_inc(consts_ready, 1)
            nc.gpsimd.iota(extra_key[:], [[1, EXTRAS]], base=1, channel_multiplier=0,
                           allow_small_or_imprecise_dtypes=True).then_inc(consts_ready, 1)
            nc.gpsimd.memset(ident[:], 0.0).then_inc(pool_step, 1)
            nc.gpsimd.memset(pair_least[:], 0.0).then_inc(pool_step, 1)
            pool.wait_ge(pool_step, 2)
            nc.gpsimd.affine_select(out=before[:], in_=before[:], compare_op=ALU.is_gt, fill=0.0,
                                    base=0, pattern=[[1, P]], channel_multiplier=-1
                                    ).then_inc(consts_ready, 1)
            keep = scan_keep[:].rearrange("p (s c) -> p s c", c=TPP)
            nc.gpsimd.affine_select(out=keep, in_=keep, compare_op=ALU.is_gt, fill=0.0, base=0,
                                    pattern=[[0, S], [1, TPP]], channel_multiplier=0
                                    ).then_inc(consts_ready, 1)
            pool.wait_ge(pool_step, 4)
            nc.gpsimd.affine_select(out=ident[:], in_=ident[:], compare_op=ALU.not_equal, fill=1.0,
                                    base=0, pattern=[[-1, P]], channel_multiplier=1
                                    ).then_inc(consts_ready, 1)
            nc.gpsimd.affine_select(out=pair_least[:], in_=pair_least[:], compare_op=ALU.is_ge,
                                    fill=-1.5e-38, base=0, pattern=[[-1, E], [1, E]],
                                    channel_multiplier=0).then_inc(consts_ready, 1)
            nc.gpsimd.memset(up_stage[:], 0.0).then_inc(consts_ready, 1)
            nc.gpsimd.memset(minus_half[:], -0.5).then_inc(consts_ready, 1)
            pool.wait_ge(consts_ready, CONSTS)

            def root(n, done, step):
                nc.gpsimd.tensor_scalar(var_eps[:], stats[:, 1:2], EPS, 1.0, ALU.add, ALU.mult
                                        ).then_inc(pool_step, 1)
                pool.wait_ge(pool_step, step)
                nc.gpsimd.tensor_tensor(rstd[:], var_eps[:], minus_half[:], ALU.pow).then_inc(done, 1)
                pool.wait_ge(done, n + 1)

            AHEAD = 3
            pool.wait_ge(rows_ready, 1)
            for q in range(ITEMS + AHEAD):
                if q < ITEMS:
                    nc.gpsimd.indirect_dma_start(
                        cols(xg, q), None, x, bass.IndirectOffsetOnAxis(row_index[:, q:q + 1], 0)
                    ).then_inc(x_landed[q], 16)
                n = q - AHEAD
                if n >= 0:
                    pool.wait_ge(stats_ready, n + 1)
                    root(n, rstd_ready, 4 + n + 1)
            LAG = 4
            for n in range(TILES + LAG):
                if n < TILES:
                    pool.wait_ge(stats2_ready, n + 1)
                    root(n, rstd2_ready, 4 + ITEMS + n + 1)
                t = n - LAG
                if t >= 0:
                    q = tile_position(t)
                    pool.wait_ge(out_ready, t + 1)
                    nc.gpsimd.indirect_dma_start(
                        out, bass.IndirectOffsetOnAxis(row_index[:, q:q + 1], 0), cols(xg, q), None
                    ).then_inc(out_stored, 16)

        @block.scalar
        def _(act_e):
            act_e.wait_ge(gates_loaded, 16)
            nc.scalar.activation(gates_t[:], gates_raw[:], ACT.Tanh).then_inc(gates_ready, 1)
            for s in range(S):
                act_e.wait_ge(ct_loaded[s], 16)
                dst = cols(ct_split, s, KC * 2 * D).rearrange("p (k h n) -> p k h n", k=KC, h=2)
                nc.scalar.activation(dst[:, :, 0, :], ct_stage[:, s % 2], ACT.Copy
                                     ).then_inc(ct_hi_ready, 1)
            act_e.wait_ge(w_loaded, 16)
            nc.scalar.activation(w_split[:, :, 0, :], w_stage[:], ACT.Copy).then_inc(w_hi_ready, 1)
            act_e.wait_ge(up_loaded, 16)
            nc.scalar.activation(up_split[:, 0], up_stage[:], ACT.Copy).then_inc(w_hi_ready, 1)

            def hT_hi(q):
                act_e.wait_ge(hT_done, q + 1)
                nc.scalar.activation(hT[:, 0], hT_ps[:], ACT.Copy).then_inc(hT_hi_ready, 1)

            def item(q, last=False):
                act_e.wait_ge(z_done, q + 1)
                nc.scalar.activation(silu[:], z_ps[:], ACT.Silu).then_inc(silu_ready, 1)
                if not last:
                    hT_hi(q + 1)
                act_e.wait_ge(actT_done, q + 1)
                nc.scalar.activation(actT[:, 0], actT_ps[:], ACT.Copy).then_inc(actT_hi_ready, 1)

            def h2T_hi(l, parity):
                act_e.wait_ge(h2T_done, l + 1)
                nc.scalar.activation(h2T[:, parity, 0], hT_ps[:], ACT.Copy).then_inc(h2T_hi_ready, 1)

            def expo(l):
                act_e.wait_ge(max_ready, l + 1)
                nc.scalar.activation(expd[:], logits[:], ACT.Exp, bias=neg_max[:],
                                     accum_out=exp_sum[:]).then_inc(exp_ready, 1)

            def hwT_hi(l):
                act_e.wait_ge(hwT_done, l + 1)
                nc.scalar.activation(hwT[:, 0], hwT_ps[:, 0:P], ACT.Copy).then_inc(hwT_hi_ready, 1)

            hT_hi(0)
            with act_e.Fori(0, ITEMS - 1) as q:
                item(q)
            q = ITEMS - 1
            act_e.wait_ge(z_done, q + 1)
            nc.scalar.activation(silu[:], z_ps[:], ACT.Silu).then_inc(silu_ready, 1)
            h2T_hi(0, 0)
            act_e.wait_ge(actT_done, q + 1)
            nc.scalar.activation(actT[:, 0], actT_ps[:], ACT.Copy).then_inc(actT_hi_ready, 1)
            h2T_hi(1, 1)

            def tile(l, parity):
                expo(l - 1)
                h2T_hi(l + 1, 1 - parity)
                hwT_hi(l - 1)

            with act_e.Fori(1, TILES - 2, 2) as l:
                tile(l, 1)
                tile(l + 1, 0)
            for l in (TILES - 1, TILES):
                expo(l - 1)
                hwT_hi(l - 1)

        @block.tensor
        def _(pe):
            pe.wait_ge(consts_ready, CONSTS)
            pe.wait_ge(totals_ready, 1)
            nc.tensor.matmul(sort_ps[:, 0:S], before[:], totals[:], start=True, stop=False)
            nc.tensor.matmul(sort_ps[:, 0:S], ones[:], totals_before[:], start=False, stop=True)
            nc.tensor.matmul(sort_ps[:, S:2 * S], ones[:], totals_before[:], start=True, stop=True
                             ).then_inc(bases_done, 1)
            pe.wait_ge(perm_in_ready, 1)
            for c in range(TPP):
                last = nc.tensor.matmul(perm_ps[:, 0:2 * ITEMS], lo_onehot[:, c, :],
                                        item_vals[:, c].rearrange("p a b -> p (a b)"),
                                        start=(c == 0), stop=(c == TPP - 1))
            last.then_inc(perm_done, 1)
            pe.wait_ge(keys_ready, 1)
            nc.tensor.matmul(lead_ps[:, 0:ITEMS], first_row[:], row_key[:], start=True, stop=True
                             ).then_inc(lead_done, 1)

            def split_product(ps, lhs, rhs, k, first, last, lhs_chunk=True):
                at = slice(k * P, (k + 1) * P)
                nc.tensor.matmul(ps, lhs[:, 0, at], rhs(0), start=first, stop=False)
                nc.tensor.matmul(ps, lhs[:, 0, at], rhs(1), start=False, stop=False)
                return nc.tensor.matmul(ps, lhs[:, 1, at], rhs(0), start=False, stop=last)

            def transpose_chunks(ps, src):
                for k in range(KC):
                    at = slice(k * P, (k + 1) * P)
                    last = nc.tensor.transpose(ps[:, at], src[:, at], ident[:])
                return last

            def expert_product(ps, lhs, key):
                for k in range(KC):
                    last = split_product(
                        ps[:], lhs,
                        lambda part: ct_split[:, bass.ds(((key * KC + k) * 2 + part) * D, D)],
                        k, k == 0, k == KC - 1)
                return last

            def key_of(q):
                return pe.value_load(key_table[0:1, bass.ds(q, 1)], min_val=0, max_val=S - 1)

            def transpose_h(q):
                pe.wait_ge(h_ready, q + 1)
                transpose_chunks(hT_ps, h).then_inc(hT_done, 1)

            def product_z(q):
                pe.wait_ge(hT_hi_ready, q + 1)
                pe.wait_ge(hT_lo_ready, q + 1)
                expert_product(z_ps, hT, key_of(q)).then_inc(z_done, 1)

            def product_y(q):
                pe.wait_ge(actT_hi_ready, q + 1)
                pe.wait_ge(actT_lo_ready, q + 1)
                expert_product(y_ps, actT, key_of(q)).then_inc(y_done, 1)

            def transpose_act(q):
                pe.wait_ge(act_ready, q + 1)
                transpose_chunks(actT_ps, act).then_inc(actT_done, 1)

            def transpose_h2(l):
                pe.wait_ge(h2_ready, l + 1)
                transpose_chunks(hT_ps, h).then_inc(h2T_done, 1)

            def ffn_chunks(l, parity, ks):
                lhs = h2T[:, parity]
                for k in ks:
                    split_product(ffn_a[parity][:, 0:NA], lhs,
                                  lambda part: w_split[:, k, part, 0:NA], k, k == 0, k == KC - 1)
                    last = split_product(ffn_b[parity][:, 0:NB], lhs,
                                         lambda part: w_split[:, k, part, NA:WN], k, k == 0, k == KC - 1)
                return last

            def ffn_begin(l, parity):
                pe.wait_ge(h2T_hi_ready, l + 1)
                pe.wait_ge(h2T_lo_ready, l + 1)
                ffn_chunks(l, parity, (0, 1))

            def transpose_hw(l):
                pe.wait_ge(hw_ready, l + 1)
                nc.tensor.transpose(hwT_ps[:, 0:P], hw[:], ident[:]).then_inc(hwT_done, 1)

            def product_up(l, parity):
                pe.wait_ge(hwT_hi_ready, l + 1)
                pe.wait_ge(hwT_lo_ready, l + 1)
                for ps, lo_col, hi_col in ((ffn_a[parity], 0, NA), (ffn_b[parity], NA, D)):
                    for left, right in ((0, 0), (0, 1), (1, 0)):
                        last = nc.tensor.matmul(ps[:, 0:hi_col - lo_col], hwT[:, left],
                                                up_split[:, right, lo_col:hi_col],
                                                start=False, stop=(left == 1), skip_group_check=True)
                last.then_inc(up_done, 1)

            transpose_h(0)
            pe.wait_ge(ct_hi_ready, S)
            pe.wait_ge(ct_lo_ready, S)
            pe.wait_ge(tables_ready, 1)
            product_z(0)
            transpose_h(1)
            transpose_act(0)
            product_z(1)
            transpose_h(2)
            product_y(0)
            transpose_act(1)
            with pe.Fori(2, ITEMS - 1) as q:
                product_z(q)
                transpose_h(q + 1)
                pe.wait_ge(x2_ready, q - 1)
                product_y(q - 1)
                transpose_act(q)
            product_z(ITEMS - 1)
            transpose_h2(0)
            pe.wait_ge(x2_ready, ITEMS - 2)
            product_y(ITEMS - 2)
            transpose_act(ITEMS - 1)
            pe.wait_ge(w_hi_ready, 2)
            pe.wait_ge(w_lo_ready, 2)
            ffn_begin(0, 0)
            transpose_h2(1)
            ffn_chunks(0, 0, (2, 3)).then_inc(ffn_done, 1)
            pe.wait_ge(x2_ready, ITEMS - 1)
            product_y(ITEMS - 1)

            def tile(l, parity, bank_used=True, ahead=True):
                if bank_used:
                    pe.wait_ge(out_ready, l - 1)
                ffn_begin(l, parity)
                if ahead:
                    transpose_h2(l + 1)
                ffn_chunks(l, parity, (2,))
                transpose_hw(l - 1)
                ffn_chunks(l, parity, (3,)).then_inc(ffn_done, 1)
                product_up(l - 1, 1 - parity)

            tile(1, 1, bank_used=False)
            with pe.Fori(2, TILES - 3, 2) as l:
                tile(l, 0)
                tile(l + 1, 1)
            tile(TILES - 2, 0)
            tile(TILES - 1, 1, ahead=False)
            transpose_hw(TILES - 1)
            product_up(TILES - 1, 1)

        @block.vector
        def _(dve):
            steps = [0]

            def after(ins):
                steps[0] += 1
                ins.then_inc(dve_step, 1)
                dve.wait_ge(dve_step, steps[0])

            tt, ts, cp = nc.vector.tensor_tensor, nc.vector.tensor_scalar, nc.vector.tensor_copy
            nc.vector.memset(ones[:], 1.0)
            nc.vector.memset(scan_ones[:], 1.0)
            nc.vector.memset(first_row[:], 0.0)
            nc.vector.memset(at_least[:, 0, :], 1.0)
            nc.vector.memset(at_least[:, S, :], 0.0)
            nc.vector.memset(totals_before[:, 0:1], 0.0)
            nc.vector.memset(weights[:, 0:1], 1.0)
            after(nc.vector.memset(hw[:], 0.0))
            nc.vector.memset(hw[:, LORA:LORA + 1], 1.0)
            after(nc.vector.memset(first_row[0:1, :], 1.0))

            dve.wait_ge(ids_loaded, 16)
            for s in range(1, S):
                last = ts(at_least[:, s, :], ids_sb[:], float(PER_EXPERT * (S - s)), None, ALU.is_lt)
            after(last)
            after(tt(onehot[:], at_least[:, 0:S, :], at_least[:, 1:S + 1, :], ALU.subtract))
            dve.wait_ge(consts_ready, CONSTS)
            after(nc.vector.tensor_tensor_scan(
                rank[:].rearrange("p s c -> p (s c)"), scan_keep[:],
                onehot[:].rearrange("p s c -> p (s c)"), 0.0, ALU.mult, ALU.add))
            cp(totals[:], rank[:, :, TPP - 1])
            nc.vector.tensor_tensor_scan(
                totals_before[:, 1:S], scan_ones[:, 1:S], rank[:, 0:S - 1, TPP - 1], 0.0,
                ALU.mult, ALU.add).then_inc(totals_ready, 1)
            after(nc.vector.tensor_reduce(no_key[:, 1, :], at_least[:, 1:S, :].rearrange("p s c -> p c s"),
                                          axis=AX.X, op=ALU.add))
            dve.wait_ge(bases_done, 1)
            after(tt(begun[:], sort_ps[:, S + 1:2 * S].unsqueeze(2).to_broadcast([P, EXTRAS, TILES - 1]),
                     tile_starts[:].unsqueeze(1).to_broadcast([P, EXTRAS, TILES - 1]), ALU.is_ge))
            nc.vector.tensor_reduce(item_tile[:, EXTRA_AT:EXTRA_AT + EXTRAS], begun[:], axis=AX.X, op=ALU.add)
            after(tt(rank[:], rank[:], sort_ps[:, 0:S].unsqueeze(2).to_broadcast([P, S, TPP]), ALU.add))
            after(tt(rank[:], rank[:], onehot[:], ALU.mult))
            after(nc.vector.tensor_reduce(slot1[:], rank[:].rearrange("p s c -> p c s"), axis=AX.X, op=ALU.add))
            after(ts(slot[:], slot1[:], -1.0, None, ALU.add))
            ts(slot_lo[:], slot[:], P - 1, None, ALU.bitwise_and)
            after(ts(slot_tile[:], slot[:], P.bit_length() - 1, None, ALU.logical_shift_right))
            after(tt(in_item[:], slot_tile[:].unsqueeze(2).to_broadcast([P, TPP, ITEMS]),
                     item_tile[:].unsqueeze(1).to_broadcast([P, TPP, ITEMS]), ALU.is_equal))
            for a in range(2):
                tt(item_vals[:, :, a, :], in_item[:],
                   no_key[:, a, :].unsqueeze(2).to_broadcast([P, TPP, ITEMS]), ALU.mult)
            tt(lo_onehot[:], iota_row[:].unsqueeze(1).to_broadcast([P, TPP, P]),
               slot_lo[:].unsqueeze(2).to_broadcast([P, TPP, P]), ALU.is_equal).then_inc(perm_in_ready, 1)
            dve.wait_ge(perm_done, 1)
            cp(row_index[:], perm_ps[:, 0:ITEMS]).then_inc(rows_ready, 1)
            cp(row_key[:], perm_ps[:, ITEMS:2 * ITEMS]).then_inc(keys_ready, 1)
            after(ts(past_extras[:], item_tile[:], float(EXTRA_AT), float(EXTRAS), ALU.is_ge, ALU.mult))
            tt(target_table[:], item_tile[:], past_extras[:], ALU.add)
            dve.wait_ge(lead_done, 1)
            after(cp(item_key[:], lead_ps[:, 0:ITEMS]))
            extra = slice(EXTRA_AT, EXTRA_AT + EXTRAS)
            after(tt(starts_inside[:], item_key[:, extra], extra_key[:], ALU.not_equal))
            after(cp(item_key[:, extra], extra_key[:]))
            cp(key_table[:], item_key[:]).then_inc(tables_ready, 1)
            after(tt(gate_mask[:], row_key[:], item_key[:], ALU.is_equal))
            after(tt(gate_mask[:, extra], gate_mask[:, extra], starts_inside[:], ALU.mult))
            dve.wait_ge(gates_ready, 1)
            after(ts(gate_mask[:], gate_mask[:], gates_t[:, 0:1], None, ALU.mult))

            def item_stats(q):
                dve.wait_ge(x_ready, q + 1)
                nc.vector.bn_stats(bn[:], cols(xg, q)).then_inc(bn_ready, 1)

            def aggregate(done):
                nc.vector.bn_aggr(stats[:], bn[:]).then_inc(done, 1)

            def item_norm(q):
                dve.wait_ge(rstd_ready, q + 1)
                ts(h[:], cols(xg, q), stats[:, 0:1], rstd[:],
                   ALU.subtract, ALU.mult).then_inc(h_ready, 1)

            def hT_lo(q):
                dve.wait_ge(hT_hi_ready, q + 1)
                tt(hT[:, 1], hT_ps[:], hT[:, 0].bitcast(F32), ALU.subtract).then_inc(hT_lo_ready, 1)

            def activate(q, bn_sem=None, bn_count=0):
                if bn_sem is not None:
                    dve.wait_ge(bn_sem, bn_count)
                dve.wait_ge(silu_ready, q + 1)
                tt(act[:], z_ps[:], silu[:], ALU.mult).then_inc(act_ready, 1)

            def actT_lo(q):
                dve.wait_ge(actT_hi_ready, q + 1)
                tt(actT[:, 1], actT_ps[:], actT[:, 0].bitcast(F32), ALU.subtract).then_inc(actT_lo_ready, 1)

            def add_product(q, target):
                dve.wait_ge(y_done, q + 1)
                rows = cols(xg, target)
                nc.vector.scalar_tensor_tensor(rows, y_ps[:], gate_mask[:, bass.ds(q, 1)], rows,
                                               ALU.mult, ALU.add).then_inc(x2_ready, 1)

            def target_of(q):
                return dve.value_load(target_table[0:1, bass.ds(q, 1)], min_val=0, max_val=ITEMS - 1)

            def ct_lo(s):
                dve.wait_ge(ct_hi_ready, s + 1)
                dst = cols(ct_split, s, KC * 2 * D).rearrange("p (k h n) -> p k h n", k=KC, h=2)
                tt(dst[:, :, 1, :], ct_stage[:, s % 2], dst[:, :, 0, :].bitcast(F32), ALU.subtract
                   ).then_inc(ct_lo_ready, 1)

            ct_lo(0)
            ct_lo(1)
            item_stats(0)
            dve.wait_ge(bn_ready, 1)
            aggregate(stats_ready)
            ct_lo(2)
            item_norm(0)
            item_stats(1)
            dve.wait_ge(bn_ready, 2)
            aggregate(stats_ready)
            ct_lo(3)
            hT_lo(0)
            item_norm(1)
            dve.wait_ge(w_hi_ready, 2)
            tt(w_split[:, :, 1, :], w_stage[:], w_split[:, :, 0, :].bitcast(F32), ALU.subtract
               ).then_inc(w_lo_ready, 1)
            tt(up_split[:, 1], up_stage[:], up_split[:, 0].bitcast(F32), ALU.subtract
               ).then_inc(w_lo_ready, 1)

            def item(q, first=False):
                item_stats(q + 2)
                activate(q, bn_ready, q + 3)
                aggregate(stats_ready)
                hT_lo(q + 1)
                item_norm(q + 2)
                if not first:
                    add_product(q - 1, target_of(q - 1))
                actT_lo(q)

            item(0, first=True)
            with dve.Fori(1, EXTRA_AT + 1) as q:
                item(q)
            dve.wait_ge(x_ready, ITEMS)
            with dve.Fori(EXTRA_AT + 1, ITEMS - 2) as q:
                dve.wait_ge(x2_ready, q - 1)
                item(q)

            def tile_stats(p):
                nc.vector.bn_stats(bn[:], cols(xg, p)).then_inc(bn2_ready, 1)

            def tile_norm(l, p):
                dve.wait_ge(rstd2_ready, l + 1)
                ts(h[:], cols(xg, p), stats[:, 0:1], rstd[:],
                   ALU.subtract, ALU.mult).then_inc(h2_ready, 1)

            def h2T_lo(l, parity):
                dve.wait_ge(h2T_hi_ready, l + 1)
                tt(h2T[:, parity, 1], hT_ps[:], h2T[:, parity, 0].bitcast(F32), ALU.subtract
                   ).then_inc(h2T_lo_ready, 1)

            RSTEPS = 7

            def route(l, parity):
                ps = ffn_b[parity]
                n = [l * RSTEPS]

                def done(ins):
                    n[0] = n[0] + 1
                    ins.then_inc(router_step, 1)
                    dve.wait_ge(router_step, n[0])

                dve.wait_ge(ffn_done, l + 1)
                done(tt(logits[:], ps[:, HR:HR + E], br[:], ALU.add))
                nc.vector.tensor_reduce(neg_max[:], logits[:], axis=AX.X, op=ALU.max, negate=True
                                        ).then_inc(max_ready, 1)
                done(tt(pair_diff[:], logits[:].unsqueeze(1).to_broadcast([P, E, E]),
                        logits[:].unsqueeze(2).to_broadcast([P, E, E]), ALU.subtract))
                done(tt(beats[:], pair_diff[:], pair_least[:], ALU.is_gt))
                done(nc.vector.tensor_reduce(beaten_by[:], beats[:], axis=AX.X, op=ALU.add))
                dve.wait_ge(exp_ready, l + 1)
                nc.vector.reciprocal(exp_inv[:], exp_sum[:]).then_inc(router_step, 1)
                n[0] = n[0] + 1
                done(nc.vector.scalar_tensor_tensor(chosen[:], beaten_by[:], float(TOP_K), expd[:],
                                                    ALU.is_lt, ALU.mult))
                done(ts(weights[:, 1:], chosen[:], exp_inv[:], None, ALU.mult))
                tt(hw[:, 0:LORA].rearrange("p (e r) -> p e r", r=R),
                   ps[:, BB:BB + LORA].rearrange("p (e r) -> p e r", r=R),
                   weights[:].unsqueeze(2).to_broadcast([P, E + 1, R]), ALU.mult).then_inc(hw_ready, 1)

            def hwT_lo(l):
                dve.wait_ge(hwT_hi_ready, l + 1)
                tt(hwT[:, 1], hwT_ps[:, 0:P], hwT[:, 0].bitcast(F32), ALU.subtract
                   ).then_inc(hwT_lo_ready, 1)

            def finish(l, p, parity):
                dve.wait_ge(up_done, l + 1)
                for ps, lo_col, hi_col in ((ffn_a[parity], 0, NA), (ffn_b[parity], NA, D)):
                    rows = xg[:, bass.ds(p * D + lo_col, hi_col - lo_col)]
                    last = nc.vector.scalar_tensor_tensor(rows, ps[:, 0:hi_col - lo_col], gates_t[:, 1:2], rows,
                                                          ALU.mult, ALU.add)
                last.then_inc(out_ready, 1)

            q = ITEMS - 2
            dve.wait_ge(x2_ready, q - 1)
            tile_stats(0)
            activate(q, bn2_ready, 1)
            aggregate(stats2_ready)
            hT_lo(q + 1)
            tile_norm(0, 0)
            add_product(q - 1, q - 1)
            actT_lo(q)
            q = ITEMS - 1
            tile_stats(1)
            activate(q, bn2_ready, 2)
            aggregate(stats2_ready)
            h2T_lo(0, 0)
            tile_norm(1, 1)
            add_product(q - 1, q - 1)
            actT_lo(q)
            tile_stats(2)
            dve.wait_ge(bn2_ready, 3)
            aggregate(stats2_ready)
            h2T_lo(1, 1)
            tile_norm(2, 2)
            dve.wait_ge(br_loaded, 16)
            add_product(q, q)

            def tile(l, parity, finish_at=None, ahead_at=None, lo=True):
                route(l - 1, 1 - parity)
                if ahead_at is not None:
                    tile_stats(ahead_at)
                    dve.wait_ge(bn2_ready, l + 3)
                if finish_at is not None:
                    finish(l - 2, finish_at, parity)
                if ahead_at is not None:
                    aggregate(stats2_ready)
                if lo:
                    h2T_lo(l + 1, 1 - parity)
                if ahead_at is not None:
                    tile_norm(l + 2, ahead_at)
                hwT_lo(l - 1)

            tile(1, 1, ahead_at=3)
            dve.wait_ge(x2_ready, ITEMS)
            with dve.Fori(2, EXTRA_AT - 3, 2) as l:
                tile(l, 0, l - 2, l + 2)
                tile(l + 1, 1, l - 1, l + 3)
            with dve.Fori(EXTRA_AT - 2, TILES - 3, 2) as l:
                tile(l, 0, l - 2, l + 2 + EXTRAS)
                tile(l + 1, 1, l - 1, l + 3 + EXTRAS)
            tile(TILES - 2, 0, tile_position(TILES - 4))
            tile(TILES - 1, 1, tile_position(TILES - 3), lo=False)
            tile(TILES, 0, tile_position(TILES - 2), lo=False)
            finish(TILES - 1, tile_position(TILES - 1), 1)


def kernel(x, itok_BxS_13_99985, ctx_2048, g_xattn, g_ffn, L0_ffn_W_base, L0_ffn_b_base, L0_ffn_A_s,
           L0_ffn_B_s, L0_ffn_A_r, L0_ffn_B_r, L0_ffn_W_router, L0_ffn_b_router):
    import concourse.bacc as bacc
    import numpy as np
    from concourse.bass_utils import run_bass_kernel_spmd

    D = x.shape[-1]
    arrays = {
        "x_rows": np.asarray(x).reshape(-1, D),
        "ids": np.asarray(itok_BxS_13_99985).reshape(-1),
        "ct": np.asarray(ctx_2048)[::-1].transpose(0, 2, 1),
        "gates": np.concatenate([np.asarray(g_xattn), np.asarray(g_ffn)]),
        "w_ffn": np.concatenate(
            [np.asarray(L0_ffn_W_base), np.asarray(L0_ffn_A_s),
             np.asarray(L0_ffn_A_r).transpose(1, 0, 2).reshape(D, -1), np.asarray(L0_ffn_W_router)], axis=1),
        "w_up": np.concatenate(
            [np.asarray(L0_ffn_B_s), np.asarray(L0_ffn_B_r).reshape(-1, D),
             np.asarray(L0_ffn_b_base)[None]], axis=0),
        "b_router": np.asarray(L0_ffn_b_router),
    }
    arrays = {name: np.ascontiguousarray(a) for name, a in arrays.items()}
    nc = bacc.Bacc("TRN2", target_bir_lowering=False, num_devices=1)
    args = [nc.dram_tensor(name, a.shape, mybir.dt.from_np(a.dtype), kind="ExternalInput").ap()
            for name, a in arrays.items()]
    out = nc.dram_tensor("out", arrays["x_rows"].shape, F32, kind="ExternalOutput").ap()
    build_block(nc, args[0], args[1], args[2], args[3], args[4], args[5], args[6], out)
    r = run_bass_kernel_spmd(nc, [arrays], core_ids=[0])
    return r.results[0]["out"].reshape(x.shape)
```

```python
from contextlib import ExitStack

import concourse.bass as bass
from concourse import mybir

ALU = mybir.AluOpType
ACT = mybir.ActivationFunctionType
AX = mybir.AxisListType
F32 = mybir.dt.float32
F32R = mybir.dt.float32r
F16 = mybir.dt.float16
I32 = mybir.dt.int32

P = 128
VOCAB = 25000
EPS = 1e-5
TOP_K = 2
EXTRA_AT = 13


def build_block(nc, x, ids, ct, gates, w_ffn, w_up, b_router, out):
    N, D = x.shape
    S = ct.shape[0]
    KC = D // P
    TILES = N // P
    EXTRAS = S - 1
    ITEMS = TILES + EXTRAS
    TPP = N // P
    PER_EXPERT = VOCAB // S
    E = b_router.shape[0]
    LORA = w_up.shape[0] - 1
    R = LORA // (E + 1)
    WN = w_ffn.shape[1]
    NA = (WN // 2 + 1) // 2 * 2
    NB = WN - NA
    BB = D - NA
    HR = BB + LORA
    assert NA <= 512 and NB <= 512 and LORA + 1 <= P and ITEMS == 19 and TILES == 16

    def tile_position(t):
        return t if t < EXTRA_AT else t + EXTRAS

    with ExitStack() as ctx:
        def sb(name, shape, dt=F32):
            return ctx.enter_context(nc.sbuf_tensor(name, shape, dt))

        def bank(name):
            return ctx.enter_context(nc.psum_tensor(name, [P, 512], F32))

        def sem(name):
            return ctx.enter_context(nc.semaphore(name))

        xg = sb("xg", [P, ITEMS * D])
        ct_split = sb("ct_split", [P, S * KC * 2 * D], F32R)
        ct_stage = sb("ct_stage", [P, S, KC, D])
        w_split = sb("w_split", [P, KC * 2 * WN], F32R)
        up_split = sb("up_split", [P, 2, D], F32R)
        w_stage = ct_stage[:, 0:2].rearrange("p s k n -> p (s k n)")[:, 0:KC * WN]
        up_stage = ct_stage[:, 2, 0, :]
        h = sb("h", [P, D])
        scaled = sb("scaled", [P, D])
        hT = sb("hT", [P, 2, D], F32R)
        silu = sb("silu", [P, D])
        act = sb("act", [P, D])
        actT = sb("actT", [P, 2, D], F32R)
        h2T = [hT, sb("h2T", [P, 2, D], F32R), actT]
        hw = sb("hw", [P, P])
        hwT = sb("hwT", [P, 2, P], F32R)
        bn = sb("bn", [P, 6])
        stats = sb("stats", [P, 2])
        rstd = sb("rstd", [P, 1])
        var_eps = sb("var_eps", [P, 1])
        minus_half = sb("minus_half", [P, 1])
        ident = sb("ident", [P, P])
        before = sb("before", [P, P], F16)
        ones = sb("ones", [P, P], F16)
        first_row = sb("first_row", [P, P], F16)
        iota_row = sb("iota_row", [P, P], F16)
        token_no = sb("token_no", [P, TPP])
        scan_keep = sb("scan_keep", [P, S * TPP])
        ids_sb = sb("ids_sb", [P, TPP], I32)
        at_least = sb("at_least", [P, S + 1, TPP])
        onehot = sb("onehot", [P, S, TPP])
        rank = sb("rank", [P, S, TPP])
        totals = sb("totals", [P, S], F16)
        totals_before = sb("totals_before", [P, S], F16)
        scan_ones = sb("scan_ones", [P, S])
        no_key = sb("no_key", [P, 2, TPP])
        slot1 = sb("slot1", [P, TPP])
        slot = sb("slot", [P, TPP], I32)
        slot_lo = sb("slot_lo", [P, TPP], I32)
        slot_tile = sb("slot_tile", [P, TPP], I32)
        tile_starts = sb("tile_starts", [P, TILES - 1])
        begun = sb("begun", [P, EXTRAS, TILES - 1])
        item_tile = sb("item_tile", [P, ITEMS])
        in_item = sb("in_item", [P, TPP, ITEMS])
        lo_onehot = sb("lo_onehot", [P, TPP, P], F16)
        item_vals = sb("item_vals", [P, TPP, 2, ITEMS], F16)
        row_index = sb("row_index", [P, ITEMS], I32)
        row_key = sb("row_key", [P, ITEMS], F16)
        item_key = sb("item_key", [P, ITEMS])
        extra_key = sb("extra_key", [P, EXTRAS])
        starts_inside = sb("starts_inside", [P, EXTRAS])
        gate_mask = sb("gate_mask", [P, ITEMS])
        past_extras = sb("past_extras", [P, ITEMS])
        key_table = sb("key_table", [P, ITEMS], I32)
        target_table = sb("target_table", [P, ITEMS], I32)
        gates_raw = sb("gates_raw", [P, 2])
        gates_t = sb("gates_t", [P, 2])
        br = sb("br", [P, E])
        logits = sb("logits", [P, E])
        neg_max = sb("neg_max", [P, 1])
        expd = sb("expd", [P, E])
        exp_sum = sb("exp_sum", [P, 1])
        exp_inv = sb("exp_inv", [P, 1])
        pair_diff = sb("pair_diff", [P, E, E])
        pair_least = sb("pair_least", [P, E, E])
        beats = sb("beats", [P, E, E])
        beaten_by = sb("beaten_by", [P, E])
        chosen = sb("chosen", [P, E])
        weights = sb("weights", [P, E + 1])

        z_ps, hT_ps, actT_ps, y_ps = bank("z_ps"), bank("hT_ps"), bank("actT_ps"), bank("y_ps")
        ffn_a = [bank("ffn_a0"), bank("ffn_a1"), z_ps]
        ffn_b = [bank("ffn_b0"), bank("ffn_b1"), y_ps]
        hwT_ps = actT_ps
        sort_ps, perm_ps, lead_ps = ffn_a[0], ffn_a[1], ffn_b[0]

        ids_loaded, gates_loaded, br_loaded = sem("ids_loaded"), sem("gates_loaded"), sem("br_loaded")
        ct_loaded = [sem(f"ct_loaded{s}") for s in range(S)]
        w_loaded, up_loaded = sem("w_loaded"), sem("up_loaded")
        x_landed = [sem(f"x_landed{q}") for q in range(ITEMS)]
        x_ready = sem("x_ready")
        out_stored = sem("out_stored")
        consts_ready = sem("consts_ready")
        pool_step = sem("pool_step")
        dve_step = sem("dve_step")
        gates_ready = sem("gates_ready")
        up_zeroed = sem("up_zeroed")
        totals_ready, bases_done = sem("totals_ready"), sem("bases_done")
        perm_in_ready, perm_done = sem("perm_in_ready"), sem("perm_done")
        rows_ready, keys_ready, lead_done, tables_ready = (
            sem("rows_ready"), sem("keys_ready"), sem("lead_done"), sem("tables_ready"))
        ct_hi_ready, ct_lo_ready = sem("ct_hi_ready"), sem("ct_lo_ready")
        w_hi_ready, w_lo_ready = sem("w_hi_ready"), sem("w_lo_ready")
        stats_ready, rstd_ready, h_ready = sem("stats_ready"), sem("rstd_ready"), sem("h_ready")
        hT_done, hT_hi_ready, hT_lo_ready = sem("hT_done"), sem("hT_hi_ready"), sem("hT_lo_ready")
        z_done, silu_ready, act_ready = sem("z_done"), sem("silu_ready"), sem("act_ready")
        actT_done, actT_hi_ready, actT_lo_ready = (
            sem("actT_done"), sem("actT_hi_ready"), sem("actT_lo_ready"))
        y_done, x2_ready = sem("y_done"), sem("x2_ready")
        stats2_ready, rstd2_ready, h2_ready = sem("stats2_ready"), sem("rstd2_ready"), sem("h2_ready")
        h2T_done, h2T_hi_ready, h2T_lo_ready = sem("h2T_done"), sem("h2T_hi_ready"), sem("h2T_lo_ready")
        ffn_done, max_ready, exp_ready = sem("ffn_done"), sem("max_ready"), sem("exp_ready")
        hw_ready, hwT_done, hwT_hi_ready, hwT_lo_ready = (
            sem("hw_ready"), sem("hwT_done"), sem("hwT_hi_ready"), sem("hwT_lo_ready"))
        up_done, scaled_ready, out_ready = sem("up_done"), sem("scaled_ready"), sem("out_ready")
        last_rows_ready = sem("last_rows_ready")
        bn_ready, bn2_ready = sem("bn_ready"), sem("bn2_ready")
        router_step = sem("router_step")
        block = ctx.enter_context(nc.Block())

        CONSTS = 11

        def cols(tensor, position, width=D):
            return tensor[:, bass.ds(position * width, width)]

        @block.sync
        def _(sp):
            sp.dma_start(ids_sb[:], ids.rearrange("(p c) -> p c", c=TPP)).then_inc(ids_loaded, 16)
            sp.dma_start(gates_raw[:], gates.partition_broadcast(P)).then_inc(gates_loaded, 16)
            for s in range(S):
                sp.dma_start(ct_stage[:, s], ct[s].rearrange("(k p) n -> p k n", p=P)).then_inc(ct_loaded[s], 16)
            sp.dma_start(br[:], b_router.partition_broadcast(P)).then_inc(br_loaded, 16)
            for q in range(ITEMS):
                sp.wait_ge(x_landed[q], 16)
                sp.sem_inc(x_ready, 1)
            sp.wait_ge(out_stored, 16 * TILES)

        @block.gpsimd
        def _(pool):
            nc.gpsimd.memset(before[:], 1.0).then_inc(pool_step, 1)
            nc.gpsimd.memset(scan_keep[:], 1.0).then_inc(pool_step, 1)
            nc.gpsimd.iota(iota_row[:], [[1, P]], base=0, channel_multiplier=0,
                           allow_small_or_imprecise_dtypes=True).then_inc(consts_ready, 1)
            nc.gpsimd.iota(no_key[:, 0, :], [[1, TPP]], base=0, channel_multiplier=TPP,
                           allow_small_or_imprecise_dtypes=True).then_inc(consts_ready, 1)
            nc.gpsimd.iota(tile_starts[:], [[P, TILES - 1]], base=P, channel_multiplier=0,
                           allow_small_or_imprecise_dtypes=True).then_inc(consts_ready, 1)
            nc.gpsimd.iota(item_tile[:, 0:EXTRA_AT], [[1, EXTRA_AT]], base=0, channel_multiplier=0,
                           allow_small_or_imprecise_dtypes=True).then_inc(consts_ready, 1)
            nc.gpsimd.iota(item_tile[:, EXTRA_AT + EXTRAS:], [[1, TILES - EXTRA_AT]], base=EXTRA_AT,
                           channel_multiplier=0,
                           allow_small_or_imprecise_dtypes=True).then_inc(consts_ready, 1)
            nc.gpsimd.iota(extra_key[:], [[1, EXTRAS]], base=1, channel_multiplier=0,
                           allow_small_or_imprecise_dtypes=True).then_inc(consts_ready, 1)
            nc.gpsimd.memset(ident[:], 0.0).then_inc(pool_step, 1)
            nc.gpsimd.memset(pair_least[:], 0.0).then_inc(pool_step, 1)
            pool.wait_ge(pool_step, 2)
            nc.gpsimd.affine_select(out=before[:], in_=before[:], compare_op=ALU.is_gt, fill=0.0,
                                    base=0, pattern=[[1, P]], channel_multiplier=-1
                                    ).then_inc(consts_ready, 1)
            keep = scan_keep[:].rearrange("p (s c) -> p s c", c=TPP)
            nc.gpsimd.affine_select(out=keep, in_=keep, compare_op=ALU.is_gt, fill=0.0, base=0,
                                    pattern=[[0, S], [1, TPP]], channel_multiplier=0
                                    ).then_inc(consts_ready, 1)
            pool.wait_ge(pool_step, 4)
            nc.gpsimd.affine_select(out=ident[:], in_=ident[:], compare_op=ALU.not_equal, fill=1.0,
                                    base=0, pattern=[[-1, P]], channel_multiplier=1
                                    ).then_inc(consts_ready, 1)
            nc.gpsimd.affine_select(out=pair_least[:], in_=pair_least[:], compare_op=ALU.is_ge,
                                    fill=-1.5e-38, base=0, pattern=[[-1, E], [1, E]],
                                    channel_multiplier=0).then_inc(consts_ready, 1)
            nc.gpsimd.memset(minus_half[:], -0.5).then_inc(consts_ready, 1)
            pool.wait_ge(consts_ready, CONSTS)

            def root(n, done, step):
                nc.gpsimd.tensor_scalar(var_eps[:], stats[:, 1:2], EPS, 1.0, ALU.add, ALU.mult
                                        ).then_inc(pool_step, 1)
                pool.wait_ge(pool_step, step)
                nc.gpsimd.tensor_tensor(rstd[:], var_eps[:], minus_half[:], ALU.pow).then_inc(done, 1)
                pool.wait_ge(done, n + 1)

            AHEAD = 3
            pool.wait_ge(rows_ready, 1)
            for q in range(ITEMS + AHEAD):
                if q < ITEMS:
                    nc.gpsimd.indirect_dma_start(
                        cols(xg, q), None, x, bass.IndirectOffsetOnAxis(row_index[:, q:q + 1], 0)
                    ).then_inc(x_landed[q], 16)
                n = q - AHEAD
                if n >= 0:
                    pool.wait_ge(stats_ready, n + 1)
                    root(n, rstd_ready, 4 + n + 1)
            LAG = 4
            for n in range(TILES + LAG):
                if n < TILES:
                    pool.wait_ge(stats2_ready, n + 1)
                    root(n, rstd2_ready, 4 + ITEMS + n + 1)
                t = n - LAG
                if t >= 0:
                    q = tile_position(t)
                    if t < TILES - 1:
                        pool.wait_ge(scaled_ready, 2 * (t + 1))
                        nc.gpsimd.tensor_tensor(cols(xg, q), scaled[:], cols(xg, q), ALU.add
                                                ).then_inc(out_ready, 1)
                        pool.wait_ge(out_ready, t + 1)
                    else:
                        pool.wait_ge(last_rows_ready, 2)
                    nc.gpsimd.indirect_dma_start(
                        out, bass.IndirectOffsetOnAxis(row_index[:, q:q + 1], 0), cols(xg, q), None
                    ).then_inc(out_stored, 16)

        @block.scalar
        def _(act_e):
            act_e.wait_ge(gates_loaded, 16)
            nc.scalar.activation(gates_t[:], gates_raw[:], ACT.Tanh).then_inc(gates_ready, 1)
            nc.scalar.preload_act_table(ACT.Silu)
            for s in range(S):
                act_e.wait_ge(ct_loaded[s], 16)
                dst = cols(ct_split, s, KC * 2 * D).rearrange("p (k h n) -> p k h n", k=KC, h=2)
                nc.scalar.activation(dst[:, :, 0, :], ct_stage[:, s], ACT.Copy).then_inc(ct_hi_ready, 1)

            def w_hi(k):
                nc.scalar.activation(w_split[:, bass.ds(k * 2 * WN, WN)], cols(w_stage, k, WN), ACT.Copy
                                     ).then_inc(w_hi_ready, 1)

            def hT_hi(q):
                act_e.wait_ge(hT_done, q + 1)
                nc.scalar.activation(hT[:, 0], hT_ps[:], ACT.Copy).then_inc(hT_hi_ready, 1)

            def item(q, last=False):
                act_e.wait_ge(z_done, q + 1)
                nc.scalar.activation(silu[:], z_ps[:], ACT.Silu).then_inc(silu_ready, 1)
                if not last:
                    hT_hi(q + 1)
                act_e.wait_ge(actT_done, q + 1)
                nc.scalar.activation(actT[:, 0], actT_ps[:], ACT.Copy).then_inc(actT_hi_ready, 1)

            def h2T_hi(l, turn):
                act_e.wait_ge(h2T_done, l + 1)
                nc.scalar.activation(h2T[turn][:, 0], hT_ps[:], ACT.Copy).then_inc(h2T_hi_ready, 1)

            def expo(l):
                act_e.wait_ge(max_ready, l + 1)
                nc.scalar.activation(expd[:], logits[:], ACT.Exp, bias=neg_max[:],
                                     accum_out=exp_sum[:]).then_inc(exp_ready, 1)

            def hwT_hi(l):
                act_e.wait_ge(hwT_done, l + 1)
                nc.scalar.activation(hwT[:, 0], hwT_ps[:, 0:P], ACT.Copy).then_inc(hwT_hi_ready, 1)

            def scale_out(l, turn):
                act_e.wait_ge(up_done, l + 1)
                for ps, lo_col, hi_col in ((ffn_a[turn], 0, NA), (ffn_b[turn], NA, D)):
                    nc.scalar.activation(scaled[:, lo_col:hi_col], ps[:, 0:hi_col - lo_col], ACT.Copy,
                                         scale=gates_t[:, 1:2]).then_inc(scaled_ready, 1)

            hT_hi(0)
            act_e.wait_ge(ct_lo_ready, 2)
            act_e.dma_start(w_stage.rearrange("p (k n) -> p k n", k=KC),
                            w_ffn.rearrange("(k p) n -> p k n", p=P)).then_inc(w_loaded, 16)
            act_e.wait_ge(up_zeroed, 1)
            act_e.dma_start(up_stage[0:LORA + 1, :], w_up).then_inc(up_loaded, 16)
            item(0)
            act_e.wait_ge(w_loaded, 16)
            with act_e.Fori(1, 1 + KC) as q:
                item(q)
                w_hi(q - 1)
            act_e.wait_ge(up_loaded, 16)
            nc.scalar.activation(up_split[:, 0], up_stage, ACT.Copy).then_inc(w_hi_ready, 1)
            with act_e.Fori(1 + KC, ITEMS - 1) as q:
                item(q)
            q = ITEMS - 1
            act_e.wait_ge(z_done, q + 1)
            nc.scalar.activation(silu[:], z_ps[:], ACT.Silu).then_inc(silu_ready, 1)
            nc.scalar.preload_act_table(ACT.Exp)
            h2T_hi(0, 0)
            act_e.wait_ge(actT_done, q + 1)
            nc.scalar.activation(actT[:, 0], actT_ps[:], ACT.Copy).then_inc(actT_hi_ready, 1)
            h2T_hi(1, 1)

            def tile(l, turn, scaled_used=True, ahead=True):
                expo(l - 1)
                if scaled_used:
                    act_e.wait_ge(out_ready, l - 2)
                scale_out(l - 2, (turn + 1) % 3)
                if ahead:
                    h2T_hi(l + 1, (turn + 1) % 3)
                hwT_hi(l - 1)

            expo(0)
            h2T_hi(2, 2)
            hwT_hi(0)
            tile(2, 2, scaled_used=False)
            with act_e.Fori(3, TILES - 3, 3) as l:
                for turn in range(3):
                    tile(l + turn, turn)
            tile(TILES - 1, 0, ahead=False)
            tile(TILES, 1, ahead=False)

        @block.tensor
        def _(pe):
            pe.wait_ge(consts_ready, CONSTS)
            pe.wait_ge(totals_ready, 1)
            nc.tensor.matmul(sort_ps[:, 0:S], before[:], totals[:], start=True, stop=False)
            nc.tensor.matmul(sort_ps[:, 0:S], ones[:], totals_before[:], start=False, stop=True)
            nc.tensor.matmul(sort_ps[:, S:2 * S], ones[:], totals_before[:], start=True, stop=True
                             ).then_inc(bases_done, 1)
            for c in range(TPP):
                pe.wait_ge(perm_in_ready, c + 1)
                last = nc.tensor.matmul(perm_ps[:, 0:2 * ITEMS], lo_onehot[:, c, :],
                                        item_vals[:, c].rearrange("p a b -> p (a b)"),
                                        start=(c == 0), stop=(c == TPP - 1))
            last.then_inc(perm_done, 1)
            pe.wait_ge(keys_ready, 1)
            nc.tensor.matmul(lead_ps[:, 0:ITEMS], first_row[:], row_key[:], start=True, stop=True
                             ).then_inc(lead_done, 1)

            def split_product(ps, lhs, rhs, k, first, last, lhs_chunk=True):
                at = slice(k * P, (k + 1) * P)
                nc.tensor.matmul(ps, lhs[:, 0, at], rhs(0), start=first, stop=False)
                nc.tensor.matmul(ps, lhs[:, 0, at], rhs(1), start=False, stop=False)
                return nc.tensor.matmul(ps, lhs[:, 1, at], rhs(0), start=False, stop=last)

            def transpose_chunks(ps, src):
                for k in range(KC):
                    at = slice(k * P, (k + 1) * P)
                    last = nc.tensor.transpose(ps[:, at], src[:, at], ident[:])
                return last

            def expert_product(ps, lhs, key):
                for k in range(KC):
                    last = split_product(
                        ps[:], lhs,
                        lambda part: ct_split[:, bass.ds(((key * KC + k) * 2 + part) * D, D)],
                        k, k == 0, k == KC - 1)
                return last

            def key_of(q):
                return pe.value_load(key_table[0:1, bass.ds(q, 1)], min_val=0, max_val=S - 1)

            def transpose_h(q):
                pe.wait_ge(h_ready, q + 1)
                transpose_chunks(hT_ps, h).then_inc(hT_done, 1)

            def product_z(q, key=None):
                pe.wait_ge(hT_hi_ready, q + 1)
                pe.wait_ge(hT_lo_ready, q + 1)
                expert_product(z_ps, hT, key_of(q) if key is None else key).then_inc(z_done, 1)

            def product_y(q):
                pe.wait_ge(actT_hi_ready, q + 1)
                pe.wait_ge(actT_lo_ready, q + 1)
                expert_product(y_ps, actT, key_of(q)).then_inc(y_done, 1)

            def transpose_act(q):
                pe.wait_ge(act_ready, q + 1)
                transpose_chunks(actT_ps, act).then_inc(actT_done, 1)

            def transpose_h2(l):
                pe.wait_ge(h2_ready, l + 1)
                transpose_chunks(hT_ps, h).then_inc(h2T_done, 1)

            def w_cols(k, part, lo_col, hi_col):
                at = (k * 2 + part) * WN
                return w_split[:, at + lo_col:at + hi_col]

            def ffn_bank_a(turn, k):
                split_product(ffn_a[turn][:, 0:NA], h2T[turn],
                              lambda part: w_cols(k, part, 0, NA), k, k == 0, k == KC - 1)

            def ffn_bank_b(turn, k):
                return split_product(ffn_b[turn][:, 0:NB], h2T[turn],
                                     lambda part: w_cols(k, part, NA, WN), k, k == 0, k == KC - 1)

            def ffn_chunk(turn, k):
                ffn_bank_a(turn, k)
                return ffn_bank_b(turn, k)

            def ffn_begin(l, turn):
                pe.wait_ge(h2T_hi_ready, l + 1)
                pe.wait_ge(h2T_lo_ready, l + 1)
                ffn_chunk(turn, 0)

            def transpose_hw(l):
                pe.wait_ge(hw_ready, l + 1)
                nc.tensor.transpose(hwT_ps[:, 0:P], hw[:], ident[:]).then_inc(hwT_done, 1)

            def product_up(l, turn):
                pe.wait_ge(hwT_hi_ready, l + 1)
                pe.wait_ge(hwT_lo_ready, l + 1)
                for ps, lo_col, hi_col in ((ffn_a[turn], 0, NA), (ffn_b[turn], NA, D)):
                    for left, right in ((0, 0), (0, 1), (1, 0)):
                        last = nc.tensor.matmul(ps[:, 0:hi_col - lo_col], hwT[:, left],
                                                up_split[:, right, lo_col:hi_col],
                                                start=False, stop=(left == 1), skip_group_check=True)
                last.then_inc(up_done, 1)

            transpose_h(0)
            pe.wait_ge(tables_ready, 1)
            key = key_of(0)
            pe.wait_ge(ct_hi_ready, key + 1)
            pe.wait_ge(ct_lo_ready, key + 1)
            product_z(0, key)
            transpose_h(1)
            transpose_act(0)
            pe.wait_ge(ct_hi_ready, S)
            pe.wait_ge(ct_lo_ready, S)
            product_z(1)
            transpose_h(2)
            product_y(0)
            transpose_act(1)
            with pe.Fori(2, ITEMS - 1) as q:
                product_z(q)
                transpose_h(q + 1)
                pe.wait_ge(x2_ready, q - 1)
                product_y(q - 1)
                transpose_act(q)
            product_z(ITEMS - 1)
            transpose_h2(0)
            pe.wait_ge(x2_ready, ITEMS - 2)
            product_y(ITEMS - 2)
            transpose_act(ITEMS - 1)
            pe.wait_ge(w_hi_ready, KC + 1)
            pe.wait_ge(w_lo_ready, KC + 1)
            ffn_begin(0, 0)
            transpose_h2(1)
            ffn_chunk(0, 1)
            ffn_chunk(0, 2)
            ffn_chunk(0, 3).then_inc(ffn_done, 1)
            pe.wait_ge(x2_ready, ITEMS - 1)
            product_y(ITEMS - 1)

            def tile(l, turn, bank_used=True, ahead=True):
                if bank_used:
                    pe.wait_ge(scaled_ready, 2 * (l - 2))
                ffn_begin(l, turn)
                if ahead:
                    transpose_h2(l + 1)
                ffn_chunk(turn, 1)
                ffn_bank_a(turn, 2)
                transpose_hw(l - 1)
                ffn_bank_b(turn, 2)
                ffn_chunk(turn, 3).then_inc(ffn_done, 1)
                product_up(l - 1, (turn + 2) % 3)

            tile(1, 1, bank_used=False)
            pe.wait_ge(x2_ready, ITEMS)
            tile(2, 2, bank_used=False)
            with pe.Fori(3, TILES - 3, 3) as l:
                for turn in range(3):
                    tile(l + turn, turn)
            tile(TILES - 1, 0, ahead=False)
            transpose_hw(TILES - 1)
            product_up(TILES - 1, 0)

        @block.vector
        def _(dve):
            steps = [0]

            def after(ins):
                steps[0] += 1
                ins.then_inc(dve_step, 1)
                dve.wait_ge(dve_step, steps[0])

            tt, ts, cp = nc.vector.tensor_tensor, nc.vector.tensor_scalar, nc.vector.tensor_copy
            nc.vector.memset(ones[:], 1.0)
            nc.vector.memset(scan_ones[:], 1.0)
            nc.vector.memset(first_row[:], 0.0)
            nc.vector.memset(at_least[:, 0, :], 1.0)
            nc.vector.memset(at_least[:, S, :], 0.0)
            nc.vector.memset(totals_before[:, 0:1], 0.0)
            nc.vector.memset(weights[:, 0:1], 1.0)
            after(nc.vector.memset(hw[:], 0.0))
            nc.vector.memset(hw[:, LORA:LORA + 1], 1.0)
            after(nc.vector.memset(first_row[0:1, :], 1.0))

            def ct_lo(s):
                dve.wait_ge(ct_hi_ready, s + 1)
                dst = cols(ct_split, s, KC * 2 * D).rearrange("p (k h n) -> p k h n", k=KC, h=2)
                tt(dst[:, :, 1, :], ct_stage[:, s], dst[:, :, 0, :].bitcast(F32), ALU.subtract
                   ).then_inc(ct_lo_ready, 1)

            dve.wait_ge(ids_loaded, 16)
            for s in range(1, S):
                last = ts(at_least[:, s, :], ids_sb[:], float(PER_EXPERT * (S - s)), None, ALU.is_lt)
            after(last)
            after(tt(onehot[:], at_least[:, 0:S, :], at_least[:, 1:S + 1, :], ALU.subtract))
            dve.wait_ge(consts_ready, CONSTS)
            after(nc.vector.tensor_tensor_scan(
                rank[:].rearrange("p s c -> p (s c)"), scan_keep[:],
                onehot[:].rearrange("p s c -> p (s c)"), 0.0, ALU.mult, ALU.add))
            cp(totals[:], rank[:, :, TPP - 1])
            nc.vector.tensor_tensor_scan(
                totals_before[:, 1:S], scan_ones[:, 1:S], rank[:, 0:S - 1, TPP - 1], 0.0,
                ALU.mult, ALU.add).then_inc(totals_ready, 1)
            after(nc.vector.tensor_reduce(no_key[:, 1, :], at_least[:, 1:S, :].rearrange("p s c -> p c s"),
                                          axis=AX.X, op=ALU.add))
            dve.wait_ge(bases_done, 1)
            after(tt(begun[:], sort_ps[:, S + 1:2 * S].unsqueeze(2).to_broadcast([P, EXTRAS, TILES - 1]),
                     tile_starts[:].unsqueeze(1).to_broadcast([P, EXTRAS, TILES - 1]), ALU.is_ge))
            nc.vector.tensor_reduce(item_tile[:, EXTRA_AT:EXTRA_AT + EXTRAS], begun[:], axis=AX.X, op=ALU.add)
            after(tt(rank[:], rank[:], sort_ps[:, 0:S].unsqueeze(2).to_broadcast([P, S, TPP]), ALU.add))
            after(tt(rank[:], rank[:], onehot[:], ALU.mult))
            after(nc.vector.tensor_reduce(slot1[:], rank[:].rearrange("p s c -> p c s"), axis=AX.X, op=ALU.add))
            after(ts(slot[:], slot1[:], -1.0, None, ALU.add))
            ts(slot_lo[:], slot[:], P - 1, None, ALU.bitwise_and)
            after(ts(slot_tile[:], slot[:], P.bit_length() - 1, None, ALU.logical_shift_right))
            after(tt(in_item[:], slot_tile[:].unsqueeze(2).to_broadcast([P, TPP, ITEMS]),
                     item_tile[:].unsqueeze(1).to_broadcast([P, TPP, ITEMS]), ALU.is_equal))
            for a in range(2):
                tt(item_vals[:, :, a, :], in_item[:],
                   no_key[:, a, :].unsqueeze(2).to_broadcast([P, TPP, ITEMS]), ALU.mult)
            for c in range(TPP):
                ts(lo_onehot[:, c, :], iota_row[:], slot_lo[:, c:c + 1], None, ALU.is_equal
                   ).then_inc(perm_in_ready, 1)
            dve.wait_ge(perm_done, 1)
            cp(row_index[:], perm_ps[:, 0:ITEMS]).then_inc(rows_ready, 1)
            cp(row_key[:], perm_ps[:, ITEMS:2 * ITEMS]).then_inc(keys_ready, 1)
            ct_lo(0)
            after(ts(past_extras[:], item_tile[:], float(EXTRA_AT), float(EXTRAS), ALU.is_ge, ALU.mult))
            tt(target_table[:], item_tile[:], past_extras[:], ALU.add)
            dve.wait_ge(lead_done, 1)
            after(cp(item_key[:], lead_ps[:, 0:ITEMS]))
            extra = slice(EXTRA_AT, EXTRA_AT + EXTRAS)
            after(tt(starts_inside[:], item_key[:, extra], extra_key[:], ALU.not_equal))
            after(cp(item_key[:, extra], extra_key[:]))
            cp(key_table[:], item_key[:]).then_inc(tables_ready, 1)
            after(tt(gate_mask[:], row_key[:], item_key[:], ALU.is_equal))
            after(tt(gate_mask[:, extra], gate_mask[:, extra], starts_inside[:], ALU.mult))
            dve.wait_ge(gates_ready, 1)
            after(ts(gate_mask[:], gate_mask[:], gates_t[:, 0:1], None, ALU.mult))

            def item_stats(q):
                dve.wait_ge(x_ready, q + 1)
                nc.vector.bn_stats(bn[:], cols(xg, q)).then_inc(bn_ready, 1)

            def aggregate(done):
                nc.vector.bn_aggr(stats[:], bn[:]).then_inc(done, 1)

            def item_norm(q):
                dve.wait_ge(rstd_ready, q + 1)
                ts(h[:], cols(xg, q), stats[:, 0:1], rstd[:],
                   ALU.subtract, ALU.mult).then_inc(h_ready, 1)

            def hT_lo(q):
                dve.wait_ge(hT_hi_ready, q + 1)
                tt(hT[:, 1], hT_ps[:], hT[:, 0].bitcast(F32), ALU.subtract).then_inc(hT_lo_ready, 1)

            def activate(q, bn_sem=None, bn_count=0):
                if bn_sem is not None:
                    dve.wait_ge(bn_sem, bn_count)
                dve.wait_ge(silu_ready, q + 1)
                tt(act[:], z_ps[:], silu[:], ALU.mult).then_inc(act_ready, 1)

            def actT_lo(q):
                dve.wait_ge(actT_hi_ready, q + 1)
                tt(actT[:, 1], actT_ps[:], actT[:, 0].bitcast(F32), ALU.subtract).then_inc(actT_lo_ready, 1)

            def add_product(q, target):
                dve.wait_ge(y_done, q + 1)
                rows = cols(xg, target)
                nc.vector.scalar_tensor_tensor(rows, y_ps[:], gate_mask[:, bass.ds(q, 1)], rows,
                                               ALU.mult, ALU.add).then_inc(x2_ready, 1)

            def target_of(q):
                return dve.value_load(target_table[0:1, bass.ds(q, 1)], min_val=0, max_val=ITEMS - 1)

            def first_rows(q):
                item_stats(q)
                dve.wait_ge(bn_ready, q + 1)
                aggregate(stats_ready)

            def w_lo(k):
                dve.wait_ge(w_hi_ready, k + 1)
                tt(w_split[:, bass.ds((k * 2 + 1) * WN, WN)], cols(w_stage, k, WN),
                   w_split[:, bass.ds(k * 2 * WN, WN)].bitcast(F32), ALU.subtract).then_inc(w_lo_ready, 1)

            first_rows(0)
            ct_lo(1)
            item_norm(0)
            first_rows(1)
            hT_lo(0)
            ct_lo(2)
            item_norm(1)
            dve.wait_ge(ct_lo_ready, 3)
            nc.vector.memset(up_stage, 0.0).then_inc(up_zeroed, 1)
            ct_lo(3)

            def item(q, first=False):
                item_stats(q + 2)
                activate(q, bn_ready, q + 3)
                aggregate(stats_ready)
                hT_lo(q + 1)
                item_norm(q + 2)
                if not first:
                    add_product(q - 1, target_of(q - 1))
                actT_lo(q)

            item(0, first=True)
            with dve.Fori(1, 1 + KC) as q:
                item(q)
                w_lo(q - 1)
            dve.wait_ge(w_hi_ready, KC + 1)
            tt(up_split[:, 1], up_stage, up_split[:, 0].bitcast(F32), ALU.subtract).then_inc(w_lo_ready, 1)
            with dve.Fori(1 + KC, EXTRA_AT + 1) as q:
                item(q)
            dve.wait_ge(x_ready, ITEMS)
            with dve.Fori(EXTRA_AT + 1, ITEMS - 2) as q:
                dve.wait_ge(x2_ready, q - 1)
                item(q)

            def tile_stats(p):
                nc.vector.bn_stats(bn[:], cols(xg, p)).then_inc(bn2_ready, 1)

            def tile_norm(l, p):
                dve.wait_ge(rstd2_ready, l + 1)
                ts(h[:], cols(xg, p), stats[:, 0:1], rstd[:],
                   ALU.subtract, ALU.mult).then_inc(h2_ready, 1)

            def h2T_lo(l, turn):
                dve.wait_ge(h2T_hi_ready, l + 1)
                tt(h2T[turn][:, 1], hT_ps[:], h2T[turn][:, 0].bitcast(F32), ALU.subtract
                   ).then_inc(h2T_lo_ready, 1)

            RSTEPS = 7

            def route(l, turn, ahead_at=None):
                ps = ffn_b[turn]
                n = [l * RSTEPS]

                def done(ins):
                    n[0] = n[0] + 1
                    ins.then_inc(router_step, 1)
                    dve.wait_ge(router_step, n[0])

                dve.wait_ge(ffn_done, l + 1)
                done(tt(logits[:], ps[:, HR:HR + E], br[:], ALU.add))
                nc.vector.tensor_reduce(neg_max[:], logits[:], axis=AX.X, op=ALU.max, negate=True
                                        ).then_inc(max_ready, 1)
                done(tt(pair_diff[:], logits[:].unsqueeze(1).to_broadcast([P, E, E]),
                        logits[:].unsqueeze(2).to_broadcast([P, E, E]), ALU.subtract))
                done(tt(beats[:], pair_diff[:], pair_least[:], ALU.is_gt))
                done(nc.vector.tensor_reduce(beaten_by[:], beats[:], axis=AX.X, op=ALU.add))
                if ahead_at is not None:
                    tile_stats(ahead_at)
                    dve.wait_ge(bn2_ready, l + 4)
                dve.wait_ge(exp_ready, l + 1)
                nc.vector.reciprocal(exp_inv[:], exp_sum[:]).then_inc(router_step, 1)
                n[0] = n[0] + 1
                done(nc.vector.scalar_tensor_tensor(chosen[:], beaten_by[:], float(TOP_K), expd[:],
                                                    ALU.is_lt, ALU.mult))
                done(ts(weights[:, 1:], chosen[:], exp_inv[:], None, ALU.mult))
                tt(hw[:, 0:LORA].rearrange("p (e r) -> p e r", r=R),
                   ps[:, BB:BB + LORA].rearrange("p (e r) -> p e r", r=R),
                   weights[:].unsqueeze(2).to_broadcast([P, E + 1, R]), ALU.mult).then_inc(hw_ready, 1)

            def hwT_lo(l):
                dve.wait_ge(hwT_hi_ready, l + 1)
                tt(hwT[:, 1], hwT_ps[:, 0:P], hwT[:, 0].bitcast(F32), ALU.subtract
                   ).then_inc(hwT_lo_ready, 1)

            q = ITEMS - 2
            dve.wait_ge(x2_ready, q - 1)
            tile_stats(0)
            activate(q, bn2_ready, 1)
            aggregate(stats2_ready)
            hT_lo(q + 1)
            tile_norm(0, 0)
            add_product(q - 1, q - 1)
            actT_lo(q)
            q = ITEMS - 1
            tile_stats(1)
            activate(q, bn2_ready, 2)
            aggregate(stats2_ready)
            h2T_lo(0, 0)
            tile_norm(1, 1)
            add_product(q - 1, q - 1)
            actT_lo(q)
            tile_stats(2)
            dve.wait_ge(bn2_ready, 3)
            aggregate(stats2_ready)
            h2T_lo(1, 1)
            tile_norm(2, 2)
            dve.wait_ge(br_loaded, 16)
            add_product(q, q)

            def tile(l, turn, ahead_at=None, lo=True):
                route(l - 1, (turn + 2) % 3, ahead_at)
                if ahead_at is not None:
                    aggregate(stats2_ready)
                if lo:
                    h2T_lo(l + 1, (turn + 1) % 3)
                hwT_lo(l - 1)
                if ahead_at is not None:
                    tile_norm(l + 2, ahead_at)

            tile(1, 1, ahead_at=3)
            dve.wait_ge(x2_ready, ITEMS)
            with dve.Fori(2, EXTRA_AT - 4, 3) as l:
                for turn in (2, 0, 1):
                    tile(l + (turn + 1) % 3, turn, l + (turn + 1) % 3 + 2)
            for l in range(EXTRA_AT - 2, TILES - 2):
                tile(l, l % 3, tile_position(l + 2))
            tile(TILES - 2, 2)
            tile(TILES - 1, 0, lo=False)
            l, q = TILES - 1, ITEMS - 1
            route(l, 0)
            hwT_lo(l)
            dve.wait_ge(up_done, l + 1)
            for ps, lo_col, hi_col in ((ffn_a[0], 0, NA), (ffn_b[0], NA, D)):
                rows = xg[:, q * D + lo_col:q * D + hi_col]
                nc.vector.scalar_tensor_tensor(rows, ps[:, 0:hi_col - lo_col], gates_t[:, 1:2], rows,
                                               ALU.mult, ALU.add).then_inc(last_rows_ready, 1)


def kernel(x, itok_BxS_13_99985, ctx_2048, g_xattn, g_ffn, L0_ffn_W_base, L0_ffn_b_base, L0_ffn_A_s,
           L0_ffn_B_s, L0_ffn_A_r, L0_ffn_B_r, L0_ffn_W_router, L0_ffn_b_router):
    import concourse.bacc as bacc
    import numpy as np
    from concourse.bass_utils import run_bass_kernel_spmd

    D = x.shape[-1]
    arrays = {
        "x_rows": np.asarray(x).reshape(-1, D),
        "ids": np.asarray(itok_BxS_13_99985).reshape(-1),
        "ct": np.asarray(ctx_2048)[::-1].transpose(0, 2, 1),
        "gates": np.concatenate([np.asarray(g_xattn), np.asarray(g_ffn)]),
        "w_ffn": np.concatenate(
            [np.asarray(L0_ffn_W_base), np.asarray(L0_ffn_A_s),
             np.asarray(L0_ffn_A_r).transpose(1, 0, 2).reshape(D, -1), np.asarray(L0_ffn_W_router)], axis=1),
        "w_up": np.concatenate(
            [np.asarray(L0_ffn_B_s), np.asarray(L0_ffn_B_r).reshape(-1, D),
             np.asarray(L0_ffn_b_base)[None]], axis=0),
        "b_router": np.asarray(L0_ffn_b_router),
    }
    arrays = {name: np.ascontiguousarray(a) for name, a in arrays.items()}
    nc = bacc.Bacc("TRN2", target_bir_lowering=False, num_devices=1)
    args = [nc.dram_tensor(name, a.shape, mybir.dt.from_np(a.dtype), kind="ExternalInput").ap()
            for name, a in arrays.items()]
    out = nc.dram_tensor("out", arrays["x_rows"].shape, F32, kind="ExternalOutput").ap()
    build_block(nc, args[0], args[1], args[2], args[3], args[4], args[5], args[6], out)
    r = run_bass_kernel_spmd(nc, [arrays], core_ids=[0])
    return r.results[0]["out"].reshape(x.shape)
```

```python
from contextlib import ExitStack

import concourse.bass as bass
from concourse import mybir

ALU = mybir.AluOpType
ACT = mybir.ActivationFunctionType
AX = mybir.AxisListType
F32 = mybir.dt.float32
F32R = mybir.dt.float32r
F16 = mybir.dt.float16
I32 = mybir.dt.int32

P = 128
VOCAB = 25000
EPS = 1e-5
TOP_K = 2
WARM_UP = 16
EXTRA_AT = 13


def build_block(nc, x, ids, ct, gates, w_ffn, w_up, b_router, out):
    N, D = x.shape
    S = ct.shape[0]
    KC = D // P
    TILES = N // P
    EXTRAS = S - 1
    ITEMS = TILES + EXTRAS
    TPP = N // P
    PER_EXPERT = VOCAB // S
    E = b_router.shape[0]
    LORA = w_up.shape[0] - 1
    R = LORA // (E + 1)
    WN = w_ffn.shape[1]
    NA = (WN // 2 + 1) // 2 * 2
    NB = WN - NA
    BB = D - NA
    HR = BB + LORA
    assert NA <= 512 and NB <= 512 and LORA + 1 <= P and ITEMS == 19 and TILES == 16

    def tile_position(t):
        return t if t < EXTRA_AT else t + EXTRAS

    with ExitStack() as ctx:
        def sb(name, shape, dt=F32):
            return ctx.enter_context(nc.sbuf_tensor(name, shape, dt))

        def bank(name):
            return ctx.enter_context(nc.psum_tensor(name, [P, 512], F32))

        def sem(name):
            return ctx.enter_context(nc.semaphore(name))

        xg = sb("xg", [P, ITEMS * D])
        ct_split = sb("ct_split", [P, S * KC * 2 * D], F32R)
        ct_stage = sb("ct_stage", [P, S, KC, D])
        w_split = sb("w_split", [P, KC * 2 * WN], F32R)
        up_split = sb("up_split", [LORA + 1, 2, D], F32R)
        w_stage = ct_stage[:, 0:2].rearrange("p s k n -> p (s k n)")[:, 0:KC * WN]
        up_stage = ct_stage[0:LORA + 1, 2, 0, :]
        h = sb("h", [P, D])
        scaled = sb("scaled", [P, D])
        hT = sb("hT", [P, 2, D], F32R)
        silu = sb("silu", [P, D])
        act = sb("act", [P, D])
        actT = sb("actT", [P, 2, D], F32R)
        hT_1 = sb("hT_1", [P, 2, D], F32R)
        h2T = [hT, hT_1, actT]
        hw = sb("hw", [P, LORA + 1])
        hwT = sb("hwT", [LORA + 1, 2, P], F32R)
        bn = sb("bn", [P, 6])
        stats = sb("stats", [P, 2])
        rstd = sb("rstd", [P, 1])
        var_eps = sb("var_eps", [P, 1])
        minus_half = sb("minus_half", [P, 1])
        gathered_mark = sb("gathered_mark", [P, 1])
        ident = sb("ident", [P, P])
        before = sb("before", [P, P], F16)
        ones = sb("ones", [P, P], F16)
        partition_no = sb("partition_no", [P, 1])
        iota_row = sb("iota_row", [P, P], F16)
        token_no = sb("token_no", [P, TPP])
        scan_keep = sb("scan_keep", [P, S * TPP])
        ids_sb = sb("ids_sb", [P, TPP], I32)
        at_least = sb("at_least", [P, S + 1, TPP])
        onehot = sb("onehot", [P, S, TPP])
        rank = sb("rank", [P, S, TPP])
        totals = sb("totals", [P, S], F16)
        totals_before = sb("totals_before", [P, S], F16)
        scan_ones = sb("scan_ones", [P, S])
        slot1 = sb("slot1", [P, TPP])
        slot = sb("slot", [P, TPP], I32)
        slot_lo = sb("slot_lo", [P, TPP], I32)
        slot_tile = sb("slot_tile", [P, TPP], I32)
        tile_starts = sb("tile_starts", [P, TILES - 1])
        begun = sb("begun", [P, EXTRAS, TILES - 1])
        item_tile = sb("item_tile", [P, ITEMS])
        in_item = sb("in_item", [P, TPP, ITEMS])
        lo_onehot = sb("lo_onehot", [P, TPP, P], F16)
        item_tokens = sb("item_tokens", [P, TPP, ITEMS], F16)
        row_index = sb("row_index", [P, ITEMS], I32)
        first_slot = sb("first_slot", [P, ITEMS])
        row_slot = sb("row_slot", [P, ITEMS])
        reached = sb("reached", [P, ITEMS, S - 1])
        row_key = sb("row_key", [P, ITEMS])
        item_key = sb("item_key", [P, ITEMS])
        extra_key = sb("extra_key", [P, EXTRAS])
        starts_inside = sb("starts_inside", [P, EXTRAS])
        gate_mask = sb("gate_mask", [P, ITEMS])
        past_extras = sb("past_extras", [P, ITEMS])
        key_table = sb("key_table", [P, ITEMS], I32)
        target_table = sb("target_table", [P, ITEMS], I32)
        gates_raw = sb("gates_raw", [P, 2])
        gates_t = sb("gates_t", [P, 2])
        br = sb("br", [P, E])
        logits = sb("logits", [P, E])
        neg_max = sb("neg_max", [P, 1])
        expd = sb("expd", [P, E])
        exp_sum = sb("exp_sum", [P, 1])
        exp_inv = sb("exp_inv", [P, 1])
        pair_diff = sb("pair_diff", [P, E, E])
        pair_least = sb("pair_least", [P, E, E])
        beats = sb("beats", [P, E, E])
        beaten_by = sb("beaten_by", [P, E])
        chosen = sb("chosen", [P, E])
        weights = sb("weights", [P, E + 1])

        z_ps, hT_ps, actT_ps, y_ps = bank("z_ps"), bank("hT_ps"), bank("actT_ps"), bank("y_ps")
        ffn_a = [bank("ffn_a0"), bank("ffn_a1"), z_ps]
        ffn_b = [bank("ffn_b0"), bank("ffn_b1"), y_ps]
        hwT_ps = actT_ps
        sort_ps, perm_ps = ffn_a[0], ffn_a[1]
        z_1_ps = ffn_b[1]
        warm_ps = ffn_b[0]

        ids_loaded, gates_loaded, br_loaded = sem("ids_loaded"), sem("gates_loaded"), sem("br_loaded")
        ct_loaded = [sem(f"ct_loaded{s}") for s in range(S)]
        w_loaded, up_loaded = sem("w_loaded"), sem("up_loaded")
        x_landed = [sem(f"x_landed{q}") for q in range(ITEMS)]
        x_ready = sem("x_ready")
        first_gathered = sem("first_gathered")
        slot_lo_ready, pool_onehots_ready = sem("slot_lo_ready"), sem("pool_onehots_ready")
        out_stored = sem("out_stored")
        consts_ready = sem("consts_ready")
        pool_step = sem("pool_step")
        dve_step = sem("dve_step")
        gates_ready = sem("gates_ready")
        totals_ready, bases_done = sem("totals_ready"), sem("bases_done")
        perm_in_ready, perm_done = sem("perm_in_ready"), sem("perm_done")
        rows_ready, tables_ready = sem("rows_ready"), sem("tables_ready")
        ct_hi_ready = sem("ct_hi_ready")
        ct_lo_ready = sem("ct_lo_ready")
        w_hi_ready, w_lo_ready = sem("w_hi_ready"), sem("w_lo_ready")
        stats_ready, rstd_ready, h_ready = sem("stats_ready"), sem("rstd_ready"), sem("h_ready")
        hT_done, hT_hi_ready, hT_lo_ready = sem("hT_done"), sem("hT_hi_ready"), sem("hT_lo_ready")
        z_done, silu_ready, act_ready = sem("z_done"), sem("silu_ready"), sem("act_ready")
        actT_done, actT_hi_ready, actT_lo_ready = (
            sem("actT_done"), sem("actT_hi_ready"), sem("actT_lo_ready"))
        y_done, x2_ready = sem("y_done"), sem("x2_ready")
        stats2_ready, rstd2_ready, h2_ready = sem("stats2_ready"), sem("rstd2_ready"), sem("h2_ready")
        h2T_done, h2T_hi_ready, h2T_lo_ready = sem("h2T_done"), sem("h2T_hi_ready"), sem("h2T_lo_ready")
        ffn_done, max_ready, exp_ready = sem("ffn_done"), sem("max_ready"), sem("exp_ready")
        hw_ready, hwT_done, hwT_hi_ready, hwT_lo_ready = (
            sem("hw_ready"), sem("hwT_done"), sem("hwT_hi_ready"), sem("hwT_lo_ready"))
        up_done, scaled_ready, out_ready = sem("up_done"), sem("scaled_ready"), sem("out_ready")
        last_rows_ready = sem("last_rows_ready")
        bn_ready, bn2_ready = sem("bn_ready"), sem("bn2_ready")
        router_step = sem("router_step")
        block = ctx.enter_context(nc.Block())

        LATE_KEY = S - 1
        DVE_ONEHOTS = TPP - 5

        def ct_half(s, half):
            ks = slice(half * KC // 2, (half + 1) * KC // 2)
            split = ct_split[:, s * KC * 2 * D:(s + 1) * KC * 2 * D].rearrange(
                "p (k h n) -> p k h n", k=KC, h=2)
            return ct_stage[:, s, ks], split[:, ks, 0, :], split[:, ks, 1, :]

        CONSTS = 12

        def cols(tensor, position, width=D):
            return tensor[:, bass.ds(position * width, width)]

        @block.sync
        def _(sp):
            sp.dma_start(ids_sb[:], ids.rearrange("(p c) -> p c", c=TPP)).then_inc(ids_loaded, 16)
            sp.dma_start(gates_raw[:], gates.partition_broadcast(P)).then_inc(gates_loaded, 16)
            for s in range(S):
                if s == LATE_KEY:
                    sp.wait_ge(first_gathered, 1)
                sp.dma_start(ct_stage[:, s], ct[s].rearrange("(k p) n -> p k n", p=P)).then_inc(ct_loaded[s], 16)
            sp.dma_start(br[:], b_router.partition_broadcast(P)).then_inc(br_loaded, 16)
            for q in range(ITEMS):
                sp.wait_ge(x_landed[q], 16)
                sp.sem_inc(x_ready, 1)
            sp.wait_ge(out_stored, 16 * TILES)

        @block.gpsimd
        def _(pool):
            nc.gpsimd.memset(before[:], 1.0).then_inc(pool_step, 1)
            nc.gpsimd.memset(scan_keep[:], 1.0).then_inc(pool_step, 1)
            nc.gpsimd.iota(iota_row[:], [[1, P]], base=0, channel_multiplier=0,
                           allow_small_or_imprecise_dtypes=True).then_inc(consts_ready, 1)
            nc.gpsimd.iota(partition_no[:], [[1, 1]], base=0, channel_multiplier=1,
                           allow_small_or_imprecise_dtypes=True).then_inc(consts_ready, 1)
            nc.gpsimd.iota(token_no[:], [[1, TPP]], base=0, channel_multiplier=TPP,
                           allow_small_or_imprecise_dtypes=True).then_inc(consts_ready, 1)
            nc.gpsimd.iota(tile_starts[:], [[P, TILES - 1]], base=P, channel_multiplier=0,
                           allow_small_or_imprecise_dtypes=True).then_inc(consts_ready, 1)
            nc.gpsimd.iota(item_tile[:, 0:EXTRA_AT], [[1, EXTRA_AT]], base=0, channel_multiplier=0,
                           allow_small_or_imprecise_dtypes=True).then_inc(consts_ready, 1)
            nc.gpsimd.iota(item_tile[:, EXTRA_AT + EXTRAS:], [[1, TILES - EXTRA_AT]], base=EXTRA_AT,
                           channel_multiplier=0,
                           allow_small_or_imprecise_dtypes=True).then_inc(consts_ready, 1)
            nc.gpsimd.iota(extra_key[:], [[1, EXTRAS]], base=1, channel_multiplier=0,
                           allow_small_or_imprecise_dtypes=True).then_inc(consts_ready, 1)
            nc.gpsimd.memset(ident[:], 0.0).then_inc(pool_step, 1)
            nc.gpsimd.memset(pair_least[:], 0.0).then_inc(pool_step, 1)
            pool.wait_ge(pool_step, 2)
            nc.gpsimd.affine_select(out=before[:], in_=before[:], compare_op=ALU.is_gt, fill=0.0,
                                    base=0, pattern=[[1, P]], channel_multiplier=-1
                                    ).then_inc(consts_ready, 1)
            keep = scan_keep[:].rearrange("p (s c) -> p s c", c=TPP)
            nc.gpsimd.affine_select(out=keep, in_=keep, compare_op=ALU.is_gt, fill=0.0, base=0,
                                    pattern=[[0, S], [1, TPP]], channel_multiplier=0
                                    ).then_inc(consts_ready, 1)
            pool.wait_ge(pool_step, 4)
            nc.gpsimd.affine_select(out=ident[:], in_=ident[:], compare_op=ALU.not_equal, fill=1.0,
                                    base=0, pattern=[[-1, P]], channel_multiplier=1
                                    ).then_inc(consts_ready, 1)
            nc.gpsimd.affine_select(out=pair_least[:], in_=pair_least[:], compare_op=ALU.is_ge,
                                    fill=-1.5e-38, base=0, pattern=[[-1, E], [1, E]],
                                    channel_multiplier=0).then_inc(consts_ready, 1)
            nc.gpsimd.memset(minus_half[:], -0.5).then_inc(consts_ready, 1)
            pool.wait_ge(consts_ready, CONSTS)

            def root(n, done, step):
                nc.gpsimd.tensor_scalar(var_eps[:], stats[:, 1:2], EPS, 1.0, ALU.add, ALU.mult
                                        ).then_inc(pool_step, 1)
                pool.wait_ge(pool_step, step)
                nc.gpsimd.tensor_tensor(rstd[:], var_eps[:], minus_half[:], ALU.pow).then_inc(done, 1)
                pool.wait_ge(done, n + 1)

            AHEAD = 4

            def gather(q):
                nc.gpsimd.indirect_dma_start(
                    cols(xg, q), None, x, bass.IndirectOffsetOnAxis(row_index[:, q:q + 1], 0)
                ).then_inc(x_landed[q], 16)

            def ct_lo(half):
                pool.wait_ge(ct_hi_ready, 2 * (S - 1) + half + 1)
                stage, hi, lo = ct_half(S - 1, half)
                if half:
                    pool.wait_ge(ct_lo_ready, S - 1)
                ins = nc.gpsimd.tensor_tensor(lo, stage, hi.bitcast(F32), ALU.subtract)
                if half:
                    ins.then_inc(ct_lo_ready, 1)

            pool.wait_ge(slot_lo_ready, 1)
            for c in range(DVE_ONEHOTS, TPP):
                nc.gpsimd.tensor_scalar(lo_onehot[:, c, :], iota_row[:], slot_lo[:, c:c + 1], None,
                                        ALU.is_equal).then_inc(pool_onehots_ready, 1)
            pool.wait_ge(rows_ready, 1)
            gather(0)
            gather(1)
            nc.gpsimd.memset(gathered_mark[:], 0.0).then_inc(first_gathered, 1)
            for q in range(2, AHEAD):
                gather(q)
            for n in range(ITEMS):
                pool.wait_ge(stats_ready, n + 1)
                root(n, rstd_ready, 4 + n + 1)
                if n == 1:
                    ct_lo(0)
                    ct_lo(1)
                else:
                    q = AHEAD + max(0, n - 1)
                    if q < ITEMS:
                        gather(q)
            LAG = 4
            for n in range(TILES + LAG):
                if n < TILES:
                    pool.wait_ge(stats2_ready, n + 1)
                    root(n, rstd2_ready, 4 + ITEMS + n + 1)
                t = n - LAG
                if t >= 0:
                    q = tile_position(t)
                    if t < TILES - 2:
                        pool.wait_ge(scaled_ready, 2 * (t + 1))
                        nc.gpsimd.tensor_tensor(cols(xg, q), scaled[:], cols(xg, q), ALU.add
                                                ).then_inc(out_ready, 1)
                        pool.wait_ge(out_ready, t + 1)
                    else:
                        pool.wait_ge(last_rows_ready, 2 * (t - TILES + 3))
                    nc.gpsimd.indirect_dma_start(
                        out, bass.IndirectOffsetOnAxis(row_index[:, q:q + 1], 0), cols(xg, q), None
                    ).then_inc(out_stored, 16)

        @block.scalar
        def _(act_e):
            act_e.wait_ge(gates_loaded, 16)
            nc.scalar.activation(gates_t[:], gates_raw[:], ACT.Tanh).then_inc(gates_ready, 1)
            nc.scalar.preload_act_table(ACT.Silu)

            def ct_hi(s, half):
                act_e.wait_ge(ct_loaded[s], 16)
                stage, hi, lo = ct_half(s, half)
                nc.scalar.activation(hi, stage, ACT.Copy).then_inc(ct_hi_ready, 1)

            def w_hi(k):
                nc.scalar.activation(w_split[:, bass.ds(k * 2 * WN, WN)], cols(w_stage, k, WN), ACT.Copy
                                     ).then_inc(w_hi_ready, 1)

            def hT_hi(q, to=hT):
                act_e.wait_ge(hT_done, q + 1)
                nc.scalar.activation(to[:, 0], hT_ps[:], ACT.Copy).then_inc(hT_hi_ready, 1)

            def silu_of(q, bank=z_ps):
                act_e.wait_ge(z_done, q + 1)
                nc.scalar.activation(silu[:], bank[:], ACT.Silu).then_inc(silu_ready, 1)

            def actT_hi(q):
                act_e.wait_ge(actT_done, q + 1)
                nc.scalar.activation(actT[:, 0], actT_ps[:], ACT.Copy).then_inc(actT_hi_ready, 1)

            def item(q):
                silu_of(q)
                hT_hi(q + 1)
                actT_hi(q)

            def h2T_hi(l, turn):
                act_e.wait_ge(h2T_done, l + 1)
                nc.scalar.activation(h2T[turn][:, 0], hT_ps[:], ACT.Copy).then_inc(h2T_hi_ready, 1)

            def expo(l):
                act_e.wait_ge(max_ready, l + 1)
                nc.scalar.activation(expd[:], logits[:], ACT.Exp, bias=neg_max[:],
                                     accum_out=exp_sum[:]).then_inc(exp_ready, 1)

            def hwT_hi(l):
                act_e.wait_ge(hwT_done, l + 1)
                nc.scalar.activation(hwT[:, 0], hwT_ps[0:LORA + 1, 0:P], ACT.Copy).then_inc(hwT_hi_ready, 1)

            def scale_out(l, turn):
                act_e.wait_ge(up_done, l + 1)
                for ps, lo_col, hi_col in ((ffn_a[turn], 0, NA), (ffn_b[turn], NA, D)):
                    nc.scalar.activation(scaled[:, lo_col:hi_col], ps[:, 0:hi_col - lo_col], ACT.Copy,
                                         scale=gates_t[:, 1:2]).then_inc(scaled_ready, 1)

            for s in range(LATE_KEY):
                ct_hi(s, 0)
                ct_hi(s, 1)
            hT_hi(0)
            ct_hi(LATE_KEY, 0)
            ct_hi(LATE_KEY, 1)
            hT_hi(1, to=hT_1)
            silu_of(0)
            actT_hi(0)
            act_e.wait_ge(ct_lo_ready, 2)
            act_e.dma_start(w_stage.rearrange("p (k n) -> p k n", k=KC),
                            w_ffn.rearrange("(k p) n -> p k n", p=P)).then_inc(w_loaded, 16)
            act_e.wait_ge(ct_lo_ready, 3)
            act_e.dma_start(up_stage, w_up).then_inc(up_loaded, 16)
            silu_of(1, z_1_ps)
            hT_hi(2)
            actT_hi(1)
            act_e.wait_ge(w_loaded, 16)
            with act_e.Fori(2, 2 + KC) as q:
                item(q)
                w_hi(q - 2)
            act_e.wait_ge(up_loaded, 16)
            nc.scalar.activation(up_split[:, 0], up_stage, ACT.Copy).then_inc(w_hi_ready, 1)
            with act_e.Fori(2 + KC, ITEMS - 1) as q:
                item(q)
            silu_of(ITEMS - 1)
            nc.scalar.preload_act_table(ACT.Exp)
            h2T_hi(0, 0)
            actT_hi(ITEMS - 1)
            h2T_hi(1, 1)

            def tile(l, turn, scaled_used=True, ahead=True):
                expo(l - 1)
                if scaled_used:
                    act_e.wait_ge(out_ready, l - 2)
                scale_out(l - 2, (turn + 1) % 3)
                if ahead:
                    h2T_hi(l + 1, (turn + 1) % 3)
                hwT_hi(l - 1)

            expo(0)
            h2T_hi(2, 2)
            hwT_hi(0)
            tile(2, 2, scaled_used=False)
            with act_e.Fori(3, TILES - 3, 3) as l:
                for turn in range(3):
                    tile(l + turn, turn)
            tile(TILES - 1, 0, ahead=False)
            expo(TILES - 1)
            hwT_hi(TILES - 1)

        @block.tensor
        def _(pe):
            pe.wait_ge(consts_ready, CONSTS)
            pe.wait_ge(totals_ready, 1)
            nc.tensor.matmul(sort_ps[:, 0:S], before[:], totals[:], start=True, stop=False)
            nc.tensor.matmul(sort_ps[:, 0:S], ones[:], totals_before[:], start=False, stop=True)
            nc.tensor.matmul(sort_ps[:, S:2 * S], ones[:], totals_before[:], start=True, stop=True
                             ).then_inc(bases_done, 1)
            for c in range(TPP):
                if c < DVE_ONEHOTS:
                    pe.wait_ge(perm_in_ready, c + 1)
                else:
                    pe.wait_ge(pool_onehots_ready, c - DVE_ONEHOTS + 1)
                last = nc.tensor.matmul(perm_ps[:, 0:ITEMS], lo_onehot[:, c, :], item_tokens[:, c],
                                        start=(c == 0), stop=(c == TPP - 1))
            last.then_inc(perm_done, 1)
            for c in range(WARM_UP):
                nc.tensor.matmul(warm_ps[:], before[:],
                                 lo_onehot[:, 0:KC, :].rearrange("p a b -> p (a b)"), start=True, stop=True)

            def hi_passes(ps, lhs, rhs, k):
                at = slice(k * P, (k + 1) * P)
                for part in (0, 1):
                    nc.tensor.matmul(ps, lhs[:, 0, at], rhs(part), start=(k == 0 and part == 0), stop=False)

            def lo_pass(ps, lhs, rhs, k):
                at = slice(k * P, (k + 1) * P)
                return nc.tensor.matmul(ps, lhs[:, 1, at], rhs(0), start=False, stop=(k == KC - 1))

            def transpose_chunks(ps, src):
                for k in range(KC):
                    at = slice(k * P, (k + 1) * P)
                    last = nc.tensor.transpose(ps[:, at], src[:, at], ident[:])
                return last

            def expert_weights(key, k):
                return lambda part: ct_split[:, bass.ds(((key * KC + k) * 2 + part) * D, D)]

            def expert_hi(ps, lhs, key):
                for k in range(KC):
                    hi_passes(ps[:], lhs, expert_weights(key, k), k)

            def expert_lo(ps, lhs, key):
                for k in range(KC):
                    last = lo_pass(ps[:], lhs, expert_weights(key, k), k)
                return last

            def key_of(q):
                return pe.value_load(key_table[0:1, bass.ds(q, 1)], min_val=0, max_val=S - 1)

            def transpose_h(q):
                pe.wait_ge(h_ready, q + 1)
                transpose_chunks(hT_ps, h).then_inc(hT_done, 1)

            def product_z(q):
                key = key_of(q)
                pe.wait_ge(ct_lo_ready, S)
                pe.wait_ge(hT_hi_ready, q + 1)
                expert_hi(z_ps, hT, key)
                pe.wait_ge(hT_lo_ready, q + 1)
                expert_lo(z_ps, hT, key).then_inc(z_done, 1)

            def product_y(q, key=None, bank_used=True, between=None):
                if key is None:
                    key = key_of(q)
                if bank_used:
                    pe.wait_ge(x2_ready, q)
                pe.wait_ge(actT_hi_ready, q + 1)
                expert_hi(y_ps, actT, key)
                if between is not None:
                    between()
                pe.wait_ge(actT_lo_ready, q + 1)
                expert_lo(y_ps, actT, key).then_inc(y_done, 1)

            def transpose_act(q):
                pe.wait_ge(act_ready, q + 1)
                transpose_chunks(actT_ps, act).then_inc(actT_done, 1)

            def transpose_h2(l):
                pe.wait_ge(h2_ready, l + 1)
                transpose_chunks(hT_ps, h).then_inc(h2T_done, 1)

            def w_cols(k, part, lo_col, hi_col):
                at = (k * 2 + part) * WN
                return w_split[:, at + lo_col:at + hi_col]

            def ffn_bank(turn, which):
                lo_col, hi_col = ((0, NA), (NA, WN))[which]
                ps = (ffn_a, ffn_b)[which][turn][:, 0:hi_col - lo_col]
                return ps, lambda k: lambda part: w_cols(k, part, lo_col, hi_col)

            BANK_A, BANK_B = 0, 1

            def ffn_hi(turn, k, banks=(BANK_A, BANK_B)):
                for which in banks:
                    ps, weights_of = ffn_bank(turn, which)
                    hi_passes(ps, h2T[turn], weights_of(k), k)

            def ffn_lo(turn, banks=(BANK_A, BANK_B), ks=range(KC)):
                for k in ks:
                    for which in banks:
                        ps, weights_of = ffn_bank(turn, which)
                        last = lo_pass(ps, h2T[turn], weights_of(k), k)
                return last

            def transpose_hw(l):
                pe.wait_ge(hw_ready, l + 1)
                nc.tensor.transpose(hwT_ps[0:LORA + 1, 0:P], hw[:], ident[:]).then_inc(hwT_done, 1)

            def product_up(l, turn, each_bank=False):
                banks = ((ffn_a[turn], 0, NA), (ffn_b[turn], NA, D))
                pe.wait_ge(hwT_hi_ready, l + 1)
                for ps, lo_col, hi_col in banks:
                    for part in (0, 1):
                        nc.tensor.matmul(ps[:, 0:hi_col - lo_col], hwT[:, 0], up_split[:, part, lo_col:hi_col],
                                         start=False, stop=False, skip_group_check=True)
                pe.wait_ge(hwT_lo_ready, l + 1)
                for ps, lo_col, hi_col in banks:
                    last = nc.tensor.matmul(ps[:, 0:hi_col - lo_col], hwT[:, 1], up_split[:, 0, lo_col:hi_col],
                                            start=False, stop=True, skip_group_check=True)
                    if each_bank and lo_col == 0:
                        last.then_inc(up_done, 1)
                last.then_inc(up_done, 1)

            transpose_h(0)
            pe.wait_ge(tables_ready, 1)
            key_0, key_1 = key_of(0), key_of(1)
            pe.wait_ge(ct_lo_ready, key_0 + 1)
            pe.wait_ge(hT_hi_ready, 1)
            expert_hi(z_ps, hT, key_0)
            transpose_h(1)
            pe.wait_ge(hT_lo_ready, 1)
            expert_lo(z_ps, hT, key_0).then_inc(z_done, 1)
            pe.wait_ge(ct_lo_ready, key_1 + 1)
            pe.wait_ge(hT_hi_ready, 2)
            expert_hi(z_1_ps, hT_1, key_1)
            transpose_act(0)
            pe.wait_ge(hT_lo_ready, 2)
            expert_lo(z_1_ps, hT_1, key_1).then_inc(z_done, 1)
            product_y(0, key_0, bank_used=False, between=lambda: transpose_h(2))
            transpose_act(1)
            with pe.Fori(2, ITEMS - 1) as q:
                product_z(q)
                transpose_h(q + 1)
                product_y(q - 1)
                transpose_act(q)
            product_z(ITEMS - 1)
            transpose_h2(0)
            product_y(ITEMS - 2)
            transpose_act(ITEMS - 1)
            pe.wait_ge(w_hi_ready, KC + 1)
            pe.wait_ge(w_lo_ready, KC + 1)
            pe.wait_ge(h2T_hi_ready, 1)
            ffn_hi(0, 0)
            ffn_hi(0, 1)
            transpose_h2(1)
            ffn_hi(0, 2)
            ffn_hi(0, 3)
            pe.wait_ge(h2T_lo_ready, 1)
            ffn_lo(0).then_inc(ffn_done, 1)
            product_y(ITEMS - 1)

            def tile(l, turn, bank_used=True):
                if bank_used:
                    pe.wait_ge(scaled_ready, 2 * (l - 2))
                pe.wait_ge(h2T_hi_ready, l + 1)
                ffn_hi(turn, 0)
                ffn_hi(turn, 1)
                transpose_h2(l + 1)
                ffn_hi(turn, 2)
                ffn_hi(turn, 3)
                transpose_hw(l - 1)
                pe.wait_ge(h2T_lo_ready, l + 1)
                ffn_lo(turn).then_inc(ffn_done, 1)
                product_up(l - 1, (turn + 2) % 3)

            tile(1, 1, bank_used=False)
            pe.wait_ge(x2_ready, ITEMS)
            tile(2, 2, bank_used=False)
            with pe.Fori(3, TILES - 3, 3) as l:
                for turn in range(3):
                    tile(l + turn, turn)
            l = TILES - 1
            pe.wait_ge(scaled_ready, 2 * (l - 2))
            pe.wait_ge(h2T_hi_ready, l + 1)
            for k in range(KC):
                ffn_hi(0, k, (BANK_B,))
            pe.wait_ge(h2T_lo_ready, l + 1)
            ffn_lo(0, (BANK_B,), range(0, 2))
            transpose_hw(l - 1)
            ffn_lo(0, (BANK_B,), range(2, KC)).then_inc(ffn_done, 1)
            ffn_hi(0, 0, (BANK_A,))
            ffn_hi(0, 1, (BANK_A,))
            ffn_hi(0, 2, (BANK_A,))
            product_up(l - 1, 2)
            ffn_hi(0, 3, (BANK_A,))
            transpose_hw(l)
            ffn_lo(0, (BANK_A,))
            product_up(l, 0, each_bank=True)

        @block.vector
        def _(dve):
            steps = [0]

            def after(ins, *meanwhile):
                steps[0] += 1
                ins.then_inc(dve_step, 1)
                dve.wait_ge(dve_step, steps[0])

            tt, ts, cp = nc.vector.tensor_tensor, nc.vector.tensor_scalar, nc.vector.tensor_copy
            nc.vector.memset(ones[:], 1.0)
            nc.vector.memset(scan_ones[:], 1.0)
            nc.vector.memset(at_least[:, 0, :], 1.0)
            nc.vector.memset(at_least[:, S, :], 0.0)
            nc.vector.memset(totals_before[:, 0:1], 0.0)
            nc.vector.memset(weights[:, 0:1], 1.0)
            nc.vector.memset(hw[:, LORA:], 1.0)

            def ct_lo(s, half):
                dve.wait_ge(ct_hi_ready, 2 * s + half + 1)
                stage, hi, lo = ct_half(s, half)
                ins = tt(lo, stage, hi.bitcast(F32), ALU.subtract)
                if half:
                    ins.then_inc(ct_lo_ready, 1)

            def reach(slots):
                return tt(reached[:], slots[:].unsqueeze(2).to_broadcast([P, ITEMS, S - 1]),
                          sort_ps[:, S + 1:2 * S].unsqueeze(1).to_broadcast([P, ITEMS, S - 1]), ALU.is_ge)

            def count_reached(keys):
                return nc.vector.tensor_reduce(keys[:], reached[:], axis=AX.X, op=ALU.add)

            dve.wait_ge(ids_loaded, 16)
            for s in range(1, S):
                last = ts(at_least[:, s, :], ids_sb[:], float(PER_EXPERT * (S - s)), None, ALU.is_lt)
            after(last)
            after(tt(onehot[:], at_least[:, 0:S, :], at_least[:, 1:S + 1, :], ALU.subtract))
            dve.wait_ge(consts_ready, CONSTS)
            after(nc.vector.tensor_tensor_scan(
                rank[:].rearrange("p s c -> p (s c)"), scan_keep[:],
                onehot[:].rearrange("p s c -> p (s c)"), 0.0, ALU.mult, ALU.add))
            cp(totals[:], rank[:, :, TPP - 1])
            nc.vector.tensor_tensor_scan(
                totals_before[:, 1:S], scan_ones[:, 1:S], rank[:, 0:S - 1, TPP - 1], 0.0,
                ALU.mult, ALU.add).then_inc(totals_ready, 1)
            dve.wait_ge(bases_done, 1)
            after(tt(begun[:], sort_ps[:, S + 1:2 * S].unsqueeze(2).to_broadcast([P, EXTRAS, TILES - 1]),
                     tile_starts[:].unsqueeze(1).to_broadcast([P, EXTRAS, TILES - 1]), ALU.is_ge))
            nc.vector.tensor_reduce(item_tile[:, EXTRA_AT:EXTRA_AT + EXTRAS], begun[:], axis=AX.X, op=ALU.add)
            after(tt(rank[:], rank[:], sort_ps[:, 0:S].unsqueeze(2).to_broadcast([P, S, TPP]), ALU.add))
            after(tt(rank[:], rank[:], onehot[:], ALU.mult),
                  ts(first_slot[:], item_tile[:], float(P), None, ALU.mult))
            after(nc.vector.tensor_reduce(slot1[:], rank[:].rearrange("p s c -> p c s"), axis=AX.X, op=ALU.add),
                  ts(past_extras[:], item_tile[:], float(EXTRA_AT), float(EXTRAS), ALU.is_ge, ALU.mult))
            after(ts(slot[:], slot1[:], -1.0, None, ALU.add),
                  reach(first_slot))
            ts(slot_lo[:], slot[:], P - 1, None, ALU.bitwise_and).then_inc(slot_lo_ready, 1)
            after(ts(slot_tile[:], slot[:], P.bit_length() - 1, None, ALU.logical_shift_right),
                  tt(target_table[:], item_tile[:], past_extras[:], ALU.add))
            after(tt(in_item[:], slot_tile[:].unsqueeze(2).to_broadcast([P, TPP, ITEMS]),
                     item_tile[:].unsqueeze(1).to_broadcast([P, TPP, ITEMS]), ALU.is_equal),
                  count_reached(item_key))
            tt(item_tokens[:], in_item[:], token_no[:].unsqueeze(2).to_broadcast([P, TPP, ITEMS]), ALU.mult)
            for c in range(DVE_ONEHOTS):
                ts(lo_onehot[:, c, :], iota_row[:], slot_lo[:, c:c + 1], None, ALU.is_equal
                   ).then_inc(perm_in_ready, 1)
            dve.wait_ge(perm_done, 1)
            cp(row_index[:], perm_ps[:, 0:ITEMS]).then_inc(rows_ready, 1)
            extra = slice(EXTRA_AT, EXTRA_AT + EXTRAS)
            dve.wait_ge(perm_in_ready, DVE_ONEHOTS)
            after(tt(starts_inside[:], item_key[:, extra], extra_key[:], ALU.not_equal),
                  ts(row_slot[:], first_slot[:], partition_no[:], None, ALU.add))
            after(cp(item_key[:, extra], extra_key[:]))
            cp(key_table[:], item_key[:]).then_inc(tables_ready, 1)
            ct_lo(0, 0)
            ct_lo(0, 1)

            def gates_of_rows():
                after(reach(row_slot))
                after(count_reached(row_key))
                after(tt(gate_mask[:], row_key[:], item_key[:], ALU.is_equal))
                after(tt(gate_mask[:, extra], gate_mask[:, extra], starts_inside[:], ALU.mult))
                dve.wait_ge(gates_ready, 1)
                after(ts(gate_mask[:], gate_mask[:], gates_t[:, 0:1], None, ALU.mult))

            def item_stats(q):
                if isinstance(q, int):
                    dve.wait_ge(x_landed[q], 16)
                else:
                    dve.wait_ge(x_ready, q + 1)
                nc.vector.bn_stats(bn[:], cols(xg, q)).then_inc(bn_ready, 1)

            def aggregate(done):
                nc.vector.bn_aggr(stats[:], bn[:]).then_inc(done, 1)

            def item_norm(q):
                dve.wait_ge(rstd_ready, q + 1)
                ts(h[:], cols(xg, q), stats[:, 0:1], rstd[:],
                   ALU.subtract, ALU.mult).then_inc(h_ready, 1)

            def hT_lo(q, to=hT):
                dve.wait_ge(hT_hi_ready, q + 1)
                tt(to[:, 1], hT_ps[:], to[:, 0].bitcast(F32), ALU.subtract).then_inc(hT_lo_ready, 1)

            def activate(q, bn_sem=None, bn_count=0, bank=z_ps):
                if bn_sem is not None:
                    dve.wait_ge(bn_sem, bn_count)
                dve.wait_ge(silu_ready, q + 1)
                tt(act[:], bank[:], silu[:], ALU.mult).then_inc(act_ready, 1)

            def actT_lo(q):
                dve.wait_ge(actT_hi_ready, q + 1)
                tt(actT[:, 1], actT_ps[:], actT[:, 0].bitcast(F32), ALU.subtract).then_inc(actT_lo_ready, 1)

            def add_product(q, target):
                dve.wait_ge(y_done, q + 1)
                rows = cols(xg, target)
                nc.vector.scalar_tensor_tensor(rows, y_ps[:], gate_mask[:, bass.ds(q, 1)], rows,
                                               ALU.mult, ALU.add).then_inc(x2_ready, 1)

            def target_of(q):
                return dve.value_load(target_table[0:1, bass.ds(q, 1)], min_val=0, max_val=ITEMS - 1)

            def first_rows(q):
                item_stats(q)
                dve.wait_ge(bn_ready, q + 1)
                aggregate(stats_ready)

            def w_lo(k):
                dve.wait_ge(w_hi_ready, k + 1)
                tt(w_split[:, bass.ds((k * 2 + 1) * WN, WN)], cols(w_stage, k, WN),
                   w_split[:, bass.ds(k * 2 * WN, WN)].bitcast(F32), ALU.subtract).then_inc(w_lo_ready, 1)

            ct_lo(1, 0)
            first_rows(0)
            ct_lo(1, 1)
            item_norm(0)
            first_rows(1)
            hT_lo(0)
            item_norm(1)
            ct_lo(2, 0)
            ct_lo(2, 1)
            hT_lo(1, to=hT_1)
            item_stats(2)
            activate(0, bn_ready, 3)
            aggregate(stats_ready)
            item_norm(2)
            actT_lo(0)

            def item(q, bank=z_ps, first=False, extra_before=False):
                item_stats(q + 2)
                activate(q, bn_ready, q + 3, bank)
                aggregate(stats_ready)
                hT_lo(q + 1)
                if first:
                    gates_of_rows()
                item_norm(q + 2)
                add_product(q - 1, target_of(q - 1) if extra_before else q - 1)
                actT_lo(q)

            item(1, bank=z_1_ps, first=True)
            with dve.Fori(2, 2 + KC) as q:
                item(q)
                w_lo(q - 2)
            dve.wait_ge(w_hi_ready, KC + 1)
            tt(up_split[:, 1], up_stage, up_split[:, 0].bitcast(F32), ALU.subtract).then_inc(w_lo_ready, 1)
            with dve.Fori(2 + KC, EXTRA_AT + 1) as q:
                item(q)
            dve.wait_ge(x_ready, ITEMS)
            with dve.Fori(EXTRA_AT + 1, ITEMS - 2) as q:
                dve.wait_ge(x2_ready, q - 1)
                item(q, extra_before=True)

            def tile_stats(p):
                nc.vector.bn_stats(bn[:], cols(xg, p)).then_inc(bn2_ready, 1)

            def tile_norm(l, p):
                dve.wait_ge(rstd2_ready, l + 1)
                ts(h[:], cols(xg, p), stats[:, 0:1], rstd[:],
                   ALU.subtract, ALU.mult).then_inc(h2_ready, 1)

            def h2T_lo(l, turn):
                dve.wait_ge(h2T_hi_ready, l + 1)
                tt(h2T[turn][:, 1], hT_ps[:], h2T[turn][:, 0].bitcast(F32), ALU.subtract
                   ).then_inc(h2T_lo_ready, 1)

            RSTEPS = 7

            def route(l, turn, ahead_at=None):
                ps = ffn_b[turn]
                n = [l * RSTEPS]

                def done(ins):
                    n[0] = n[0] + 1
                    ins.then_inc(router_step, 1)
                    dve.wait_ge(router_step, n[0])

                dve.wait_ge(ffn_done, l + 1)
                done(tt(logits[:], ps[:, HR:HR + E], br[:], ALU.add))
                nc.vector.tensor_reduce(neg_max[:], logits[:], axis=AX.X, op=ALU.max, negate=True
                                        ).then_inc(max_ready, 1)
                done(tt(pair_diff[:], logits[:].unsqueeze(1).to_broadcast([P, E, E]),
                        logits[:].unsqueeze(2).to_broadcast([P, E, E]), ALU.subtract))
                done(tt(beats[:], pair_diff[:], pair_least[:], ALU.is_gt))
                done(nc.vector.tensor_reduce(beaten_by[:], beats[:], axis=AX.X, op=ALU.add))
                if ahead_at is not None:
                    tile_stats(ahead_at)
                    dve.wait_ge(bn2_ready, l + 4)
                dve.wait_ge(exp_ready, l + 1)
                nc.vector.reciprocal(exp_inv[:], exp_sum[:]).then_inc(router_step, 1)
                n[0] = n[0] + 1
                done(nc.vector.scalar_tensor_tensor(chosen[:], beaten_by[:], float(TOP_K), expd[:],
                                                    ALU.is_lt, ALU.mult))
                done(ts(weights[:, 1:], chosen[:], exp_inv[:], None, ALU.mult))
                tt(hw[:, 0:LORA].rearrange("p (e r) -> p e r", r=R),
                   ps[:, BB:BB + LORA].rearrange("p (e r) -> p e r", r=R),
                   weights[:].unsqueeze(2).to_broadcast([P, E + 1, R]), ALU.mult).then_inc(hw_ready, 1)

            def hwT_lo(l):
                dve.wait_ge(hwT_hi_ready, l + 1)
                tt(hwT[:, 1], hwT_ps[0:LORA + 1, 0:P], hwT[:, 0].bitcast(F32), ALU.subtract
                   ).then_inc(hwT_lo_ready, 1)

            q = ITEMS - 2
            dve.wait_ge(x2_ready, q - 1)
            tile_stats(0)
            activate(q, bn2_ready, 1)
            aggregate(stats2_ready)
            hT_lo(q + 1)
            tile_norm(0, 0)
            add_product(q - 1, q - 1)
            actT_lo(q)
            q = ITEMS - 1
            tile_stats(1)
            activate(q, bn2_ready, 2)
            aggregate(stats2_ready)
            h2T_lo(0, 0)
            tile_norm(1, 1)
            add_product(q - 1, q - 1)
            actT_lo(q)
            tile_stats(2)
            dve.wait_ge(bn2_ready, 3)
            aggregate(stats2_ready)
            h2T_lo(1, 1)
            tile_norm(2, 2)

            def tile(l, turn, ahead_at=None, lo=True, add_item=None):
                route(l - 1, (turn + 2) % 3, ahead_at)
                if add_item is not None:
                    add_product(add_item, add_item)
                if ahead_at is not None:
                    aggregate(stats2_ready)
                if lo:
                    h2T_lo(l + 1, (turn + 1) % 3)
                hwT_lo(l - 1)
                if ahead_at is not None:
                    tile_norm(l + 2, ahead_at)

            dve.wait_ge(br_loaded, 16)
            tile(1, 1, ahead_at=3, add_item=ITEMS - 1)
            dve.wait_ge(x2_ready, ITEMS)
            with dve.Fori(2, EXTRA_AT - 4, 3) as l:
                for turn in (2, 0, 1):
                    tile(l + (turn + 1) % 3, turn, l + (turn + 1) % 3 + 2)
            for l in range(EXTRA_AT - 2, TILES - 2):
                tile(l, l % 3, tile_position(l + 2))
            tile(TILES - 2, 2)
            tile(TILES - 1, 0, lo=False)
            def add_up(l, turn, each_bank=False):
                dve.wait_ge(up_done, l + 1)
                q = tile_position(l)
                for ps, lo_col, hi_col in ((ffn_a[turn], 0, NA), (ffn_b[turn], NA, D)):
                    if each_bank and lo_col > 0:
                        dve.wait_ge(up_done, l + 2)
                    rows = xg[:, q * D + lo_col:q * D + hi_col]
                    nc.vector.scalar_tensor_tensor(rows, ps[:, 0:hi_col - lo_col], gates_t[:, 1:2], rows,
                                                   ALU.mult, ALU.add).then_inc(last_rows_ready, 1)

            route(TILES - 1, 0)
            add_up(TILES - 2, 2)
            hwT_lo(TILES - 1)
            add_up(TILES - 1, 0, each_bank=True)


def kernel(x, itok_BxS_13_99985, ctx_2048, g_xattn, g_ffn, L0_ffn_W_base, L0_ffn_b_base, L0_ffn_A_s,
           L0_ffn_B_s, L0_ffn_A_r, L0_ffn_B_r, L0_ffn_W_router, L0_ffn_b_router):
    import concourse.bacc as bacc
    import numpy as np
    from concourse.bass_utils import run_bass_kernel_spmd

    D = x.shape[-1]
    arrays = {
        "x_rows": np.asarray(x).reshape(-1, D),
        "ids": np.asarray(itok_BxS_13_99985).reshape(-1),
        "ct": np.asarray(ctx_2048)[::-1].transpose(0, 2, 1),
        "gates": np.concatenate([np.asarray(g_xattn), np.asarray(g_ffn)]),
        "w_ffn": np.concatenate(
            [np.asarray(L0_ffn_W_base), np.asarray(L0_ffn_A_s),
             np.asarray(L0_ffn_A_r).transpose(1, 0, 2).reshape(D, -1), np.asarray(L0_ffn_W_router)], axis=1),
        "w_up": np.concatenate(
            [np.asarray(L0_ffn_B_s), np.asarray(L0_ffn_B_r).reshape(-1, D),
             np.asarray(L0_ffn_b_base)[None]], axis=0),
        "b_router": np.asarray(L0_ffn_b_router),
    }
    arrays = {name: np.ascontiguousarray(a) for name, a in arrays.items()}
    nc = bacc.Bacc("TRN2", target_bir_lowering=False, num_devices=1)
    args = [nc.dram_tensor(name, a.shape, mybir.dt.from_np(a.dtype), kind="ExternalInput").ap()
            for name, a in arrays.items()]
    out = nc.dram_tensor("out", arrays["x_rows"].shape, F32, kind="ExternalOutput").ap()
    build_block(nc, args[0], args[1], args[2], args[3], args[4], args[5], args[6], out)
    r = run_bass_kernel_spmd(nc, [arrays], core_ids=[0])
    return r.results[0]["out"].reshape(x.shape)
```
